# Optimizing a Trainium2 kernel written in Bass

```python
import numpy as np
import jax
import jax.numpy as jnp

def _softmax(x, axis=-1):
    return jax.nn.softmax(x, axis=axis)

def _gelu(x):
    return jax.nn.gelu(x, approximate=True)

def _silu(x):
    return jax.nn.silu(x)

def _sigmoid(x):
    return jax.nn.sigmoid(x)

def _layernorm(x, axis=-1, eps=1e-05):
    m = jnp.mean(x, axis=axis, keepdims=True)
    v = jnp.var(x, axis=axis, keepdims=True)
    return (x - m) / jnp.sqrt(v + eps)

def _scatter_add(tgt, idx, src, axis=0):
    return tgt.at[idx].add(src)

def _segment_sum(src, seg, n):
    return jax.ops.segment_sum(src, seg, n)
kernel_name = 'mk_recurrent_d1_jaxref_r8_a39bca'

def setup_inputs(seed: int=0):
    np.random.seed(seed)
    _w = jnp.asarray

    def _L0_attn_setup():
        import jax, jax.numpy as jnp
        import numpy as np
        B, S, HID = (1, 128, 256)
        H, DQK, DV = (16, 128, 128)
        K = 4
        SCALE = DQK ** (-0.5)

        def _dwconv_causal(x_btc, wk, bk, seq):
            y = jax.lax.conv_general_dilated(x_btc.transpose(0, 2, 1), wk, (1,), [(K - 1, K - 1)], dimension_numbers=('NCH', 'OIH', 'NCH'), feature_group_count=wk.shape[0])
            return (y[:, :, :seq] + bk[None, :, None]).transpose(0, 2, 1)

        def _kda_forward(x, Wq, Wk, Wv, Wa, ba, Wb, bb, Wg, Wo, qc_w, qc_b, kc_w, kc_b, vc_w, vc_b, ln_g, ln_b):
            Bb, Ss, _ = x.shape
            q = x @ Wq.T
            k = x @ Wk.T
            v = x @ Wv.T
            q = jax.nn.silu(_dwconv_causal(q, qc_w, qc_b, Ss))
            k = jax.nn.silu(_dwconv_causal(k, kc_w, kc_b, Ss))
            v = jax.nn.silu(_dwconv_causal(v, vc_w, vc_b, Ss))
            q = q.reshape(Bb, Ss, H, DQK)
            k = k.reshape(Bb, Ss, H, DQK) * SCALE
            v = v.reshape(Bb, Ss, H, DV)
            a = jax.nn.sigmoid(x @ Wa.T + ba).reshape(Bb, Ss, H, DV)
            beta = jax.nn.sigmoid(x @ Wb.T + bb)

            def step(St, inp):
                kt, qt, vt, at, bt = inp
                Sk = jnp.einsum('bhij,bhj->bhi', St, kt)
                err = Sk - vt
                Sn = at[..., None] * St - (bt[..., None] * err)[..., None] * kt[:, :, None, :]
                ot = jnp.einsum('bhij,bhj->bhi', Sn, qt)
                return (Sn, ot)
            tfirst = lambda u: u.transpose(1, 0, 2, 3)
            S0 = jnp.zeros((Bb, H, DV, DQK), x.dtype)
            _, outs = jax.lax.scan(step, S0, (tfirst(k), tfirst(q), tfirst(v), tfirst(a), beta.transpose(1, 0, 2)))
            out = outs.transpose(1, 0, 2, 3)
            mu = out.mean(-1, keepdims=True)
            var = out.var(-1, keepdims=True)
            o = (out - mu) * jax.lax.rsqrt(var + 1e-05) * ln_g + ln_b
            g = jax.nn.sigmoid(x @ Wg.T).reshape(Bb, Ss, H, DV)
            o = (o * g).reshape(Bb, Ss, H * DV)
            return o @ Wo.T
        key = jax.random.key(seed)
        ks = jax.random.split(key, 12)
        w = lambda i, shape, sc=0.02: jax.random.normal(ks[i], shape, jnp.float32) * sc
        return dict(x=jax.random.normal(ks[0], (B, S, HID), jnp.float32), Wq=w(1, (H * DQK, HID)), Wk=w(2, (H * DQK, HID)), Wv=w(3, (H * DV, HID)), Wa=w(4, (H * DV, HID)), ba=jnp.zeros((H * DV,), jnp.float32), Wb=w(5, (H, HID)), bb=jnp.zeros((H,), jnp.float32), Wg=w(6, (H * DV, HID)), Wo=w(7, (HID, H * DV)), qc_w=w(8, (H * DQK, 1, K), 0.2), qc_b=jnp.zeros((H * DQK,), jnp.float32), kc_w=w(9, (H * DQK, 1, K), 0.2), kc_b=jnp.zeros((H * DQK,), jnp.float32), vc_w=w(10, (H * DV, 1, K), 0.2), vc_b=jnp.zeros((H * DV,), jnp.float32), ln_g=jnp.ones((DV,), jnp.float32), ln_b=jnp.zeros((DV,), jnp.float32))
    _L0_attn_in = _L0_attn_setup()

    def _L0_ffn_setup():
        import jax, jax.numpy as jnp
        import numpy as np
        H = 256
        I = 1024
        MI = 128
        E = 8
        K = 2
        B, S = (2, 128)
        EPS = 1e-06
        ROOT = H ** (-0.5)

        def _rms(x, w=None, eps=EPS):
            ms = jnp.mean(x * x, axis=-1, keepdims=True) + eps
            y = x * jax.lax.rsqrt(ms)
            return y * w if w is not None else y

        def _gelu_tanh(x):
            return jax.nn.gelu(x, approximate=True)
        key = jax.random.key(seed)
        ks = jax.random.split(key, 10)
        s = 0.02
        return {'hidden_states': jax.random.normal(ks[0], (B, S, H), jnp.float32), 'rn_pre1': jnp.ones((H,), jnp.float32), 'rn_pre2': jnp.ones((H,), jnp.float32), 'rn_post1': jnp.ones((H,), jnp.float32), 'rn_post2': jnp.ones((H,), jnp.float32), 'rn_post': jnp.ones((H,), jnp.float32), 'w_gate': jax.random.normal(ks[1], (H, I), jnp.float32) * s, 'w_up': jax.random.normal(ks[2], (H, I), jnp.float32) * s, 'w_down': jax.random.normal(ks[3], (I, H), jnp.float32) * s, 'router_w': jax.random.normal(ks[4], (H, E), jnp.float32) * s, 'router_scale': jnp.ones((H,), jnp.float32), 'per_expert_scale': jnp.ones((E,), jnp.float32), 'we_gate': jax.random.normal(ks[5], (E, H, MI), jnp.float32) * s, 'we_up': jax.random.normal(ks[6], (E, H, MI), jnp.float32) * s, 'we_down': jax.random.normal(ks[7], (E, MI, H), jnp.float32) * s}
    _L0_ffn_in = _L0_ffn_setup()
    _d = {'L0_attn_x': _L0_attn_in['x'], 'L0_attn_Wq': _L0_attn_in['Wq'], 'L0_attn_Wk': _L0_attn_in['Wk'], 'L0_attn_Wv': _L0_attn_in['Wv'], 'L0_attn_Wa': _L0_attn_in['Wa'], 'L0_attn_ba': _L0_attn_in['ba'], 'L0_attn_Wb': _L0_attn_in['Wb'], 'L0_attn_bb': _L0_attn_in['bb'], 'L0_attn_Wg': _L0_attn_in['Wg'], 'L0_attn_Wo': _L0_attn_in['Wo'], 'L0_attn_qc_w': _L0_attn_in['qc_w'], 'L0_attn_qc_b': _L0_attn_in['qc_b'], 'L0_attn_kc_w': _L0_attn_in['kc_w'], 'L0_attn_kc_b': _L0_attn_in['kc_b'], 'L0_attn_vc_w': _L0_attn_in['vc_w'], 'L0_attn_vc_b': _L0_attn_in['vc_b'], 'L0_attn_ln_g': _L0_attn_in['ln_g'], 'L0_attn_ln_b': _L0_attn_in['ln_b'], 'L0_ffn_rn_pre1': _L0_ffn_in['rn_pre1'], 'L0_ffn_rn_pre2': _L0_ffn_in['rn_pre2'], 'L0_ffn_rn_post1': _L0_ffn_in['rn_post1'], 'L0_ffn_rn_post2': _L0_ffn_in['rn_post2'], 'L0_ffn_rn_post': _L0_ffn_in['rn_post'], 'L0_ffn_w_gate': _L0_ffn_in['w_gate'], 'L0_ffn_w_up': _L0_ffn_in['w_up'], 'L0_ffn_w_down': _L0_ffn_in['w_down'], 'L0_ffn_router_w': _L0_ffn_in['router_w'], 'L0_ffn_router_scale': _L0_ffn_in['router_scale'], 'L0_ffn_per_expert_scale': _L0_ffn_in['per_expert_scale'], 'L0_ffn_we_gate': _L0_ffn_in['we_gate'], 'L0_ffn_we_up': _L0_ffn_in['we_up'], 'L0_ffn_we_down': _L0_ffn_in['we_down']}
    _x0 = _d['L0_attn_x']
    _d['L0_attn_x'] = jax.random.normal(jax.random.fold_in(jax.random.key(seed), 1), (2, 2048, 256), dtype=_x0.dtype)
    del _x0
    return _d

def reference(L0_attn_x, L0_attn_Wq, L0_attn_Wk, L0_attn_Wv, L0_attn_Wa, L0_attn_ba, L0_attn_Wb, L0_attn_bb, L0_attn_Wg, L0_attn_Wo, L0_attn_qc_w, L0_attn_qc_b, L0_attn_kc_w, L0_attn_kc_b, L0_attn_vc_w, L0_attn_vc_b, L0_attn_ln_g, L0_attn_ln_b, L0_ffn_rn_pre1, L0_ffn_rn_pre2, L0_ffn_rn_post1, L0_ffn_rn_post2, L0_ffn_rn_post, L0_ffn_w_gate, L0_ffn_w_up, L0_ffn_w_down, L0_ffn_router_w, L0_ffn_router_scale, L0_ffn_per_expert_scale, L0_ffn_we_gate, L0_ffn_we_up, L0_ffn_we_down):

    def _L0_attn_ref(x, Wq, Wk, Wv, Wa, ba, Wb, bb, Wg, Wo, qc_w, qc_b, kc_w, kc_b, vc_w, vc_b, ln_g, ln_b):
        import jax, jax.numpy as jnp
        import numpy as np
        B, S, HID = (1, 128, 256)
        H, DQK, DV = (16, 128, 128)
        K = 4
        SCALE = DQK ** (-0.5)

        def _dwconv_causal(x_btc, wk, bk, seq):
            y = jax.lax.conv_general_dilated(x_btc.transpose(0, 2, 1), wk, (1,), [(K - 1, K - 1)], dimension_numbers=('NCH', 'OIH', 'NCH'), feature_group_count=wk.shape[0])
            return (y[:, :, :seq] + bk[None, :, None]).transpose(0, 2, 1)

        def _kda_forward(x, Wq, Wk, Wv, Wa, ba, Wb, bb, Wg, Wo, qc_w, qc_b, kc_w, kc_b, vc_w, vc_b, ln_g, ln_b):
            Bb, Ss, _ = x.shape
            q = x @ Wq.T
            k = x @ Wk.T
            v = x @ Wv.T
            q = jax.nn.silu(_dwconv_causal(q, qc_w, qc_b, Ss))
            k = jax.nn.silu(_dwconv_causal(k, kc_w, kc_b, Ss))
            v = jax.nn.silu(_dwconv_causal(v, vc_w, vc_b, Ss))
            q = q.reshape(Bb, Ss, H, DQK)
            k = k.reshape(Bb, Ss, H, DQK) * SCALE
            v = v.reshape(Bb, Ss, H, DV)
            a = jax.nn.sigmoid(x @ Wa.T + ba).reshape(Bb, Ss, H, DV)
            beta = jax.nn.sigmoid(x @ Wb.T + bb)

            def step(St, inp):
                kt, qt, vt, at, bt = inp
                Sk = jnp.einsum('bhij,bhj->bhi', St, kt)
                err = Sk - vt
                Sn = at[..., None] * St - (bt[..., None] * err)[..., None] * kt[:, :, None, :]
                ot = jnp.einsum('bhij,bhj->bhi', Sn, qt)
                return (Sn, ot)
            tfirst = lambda u: u.transpose(1, 0, 2, 3)
            S0 = jnp.zeros((Bb, H, DV, DQK), x.dtype)
            _, outs = jax.lax.scan(step, S0, (tfirst(k), tfirst(q), tfirst(v), tfirst(a), beta.transpose(1, 0, 2)))
            out = outs.transpose(1, 0, 2, 3)
            mu = out.mean(-1, keepdims=True)
            var = out.var(-1, keepdims=True)
            o = (out - mu) * jax.lax.rsqrt(var + 1e-05) * ln_g + ln_b
            g = jax.nn.sigmoid(x @ Wg.T).reshape(Bb, Ss, H, DV)
            o = (o * g).reshape(Bb, Ss, H * DV)
            return o @ Wo.T
        return _kda_forward(x, Wq, Wk, Wv, Wa, ba, Wb, bb, Wg, Wo, qc_w, qc_b, kc_w, kc_b, vc_w, vc_b, ln_g, ln_b)

    def _L0_ffn_ref(hidden_states, rn_pre1, rn_pre2, rn_post1, rn_post2, rn_post, w_gate, w_up, w_down, router_w, router_scale, per_expert_scale, we_gate, we_up, we_down):
        import jax, jax.numpy as jnp
        import numpy as np
        H = 256
        I = 1024
        MI = 128
        E = 8
        K = 2
        B, S = (2, 128)
        EPS = 1e-06
        ROOT = H ** (-0.5)

        def _rms(x, w=None, eps=EPS):
            ms = jnp.mean(x * x, axis=-1, keepdims=True) + eps
            y = x * jax.lax.rsqrt(ms)
            return y * w if w is not None else y

        def _gelu_tanh(x):
            return jax.nn.gelu(x, approximate=True)
        b, s, h = hidden_states.shape
        T = b * s
        dense_in = _rms(hidden_states, rn_pre1)
        dense_out = _gelu_tanh(dense_in @ w_gate) * (dense_in @ w_up) @ w_down
        dense_out = _rms(dense_out, rn_post1)
        x = hidden_states.reshape(T, h)
        xr = _rms(x) * router_scale * ROOT
        router_logits = xr @ router_w
        probs = jax.nn.softmax(router_logits, axis=-1)
        top_w, top_i = jax.lax.top_k(probs, K)
        top_w = top_w / jnp.sum(top_w, axis=-1, keepdims=True)
        top_w = top_w * per_expert_scale[top_i]
        aff = jnp.zeros((T, E), x.dtype).at[jnp.arange(T)[:, None], top_i].set(top_w)
        moe_in = _rms(hidden_states, rn_pre2).reshape(T, h)
        g = jnp.einsum('th,ehm->tem', moe_in, we_gate)
        u = jnp.einsum('th,ehm->tem', moe_in, we_up)
        eo = jnp.einsum('tem,emh->teh', _gelu_tanh(g) * u, we_down)
        moe_out = jnp.einsum('te,teh->th', aff, eo).reshape(b, s, h)
        moe_out = _rms(moe_out, rn_post2)
        return _rms(dense_out + moe_out, rn_post)
    x = L0_attn_x
    xn = _layernorm(x, axis=-1)
    s = _L0_attn_ref(xn, L0_attn_Wq, L0_attn_Wk, L0_attn_Wv, L0_attn_Wa, L0_attn_ba, L0_attn_Wb, L0_attn_bb, L0_attn_Wg, L0_attn_Wo, L0_attn_qc_w, L0_attn_qc_b, L0_attn_kc_w, L0_attn_kc_b, L0_attn_vc_w, L0_attn_vc_b, L0_attn_ln_g, L0_attn_ln_b)
    g = _silu(_L0_ffn_ref(xn, L0_ffn_rn_pre1, L0_ffn_rn_pre2, L0_ffn_rn_post1, L0_ffn_rn_post2, L0_ffn_rn_post, L0_ffn_w_gate, L0_ffn_w_up, L0_ffn_w_down, L0_ffn_router_w, L0_ffn_router_scale, L0_ffn_per_expert_scale, L0_ffn_we_gate, L0_ffn_we_up, L0_ffn_we_down))
    x = x + s * g
    return x

_drawn_inputs = setup_inputs


def setup_inputs(seed=0):
    import zlib

    import numpy as np

    out = dict(_drawn_inputs(seed))
    spreads = {'L0_attn_ba': (0.0, 0.8),
     'L0_attn_bb': (0.0, 0.8),
     'L0_attn_qc_b': (0.0, 0.333),
     'L0_attn_kc_b': (0.0, 0.289),
     'L0_attn_vc_b': (0.0, 0.298),
     'L0_attn_ln_g': (1.0, 0.6),
     'L0_attn_ln_b': (0.0, 0.1),
     'L0_ffn_rn_pre1': (1.0, 0.6),
     'L0_ffn_rn_pre2': (1.0, 0.6),
     'L0_ffn_rn_post1': (1.0, 0.6),
     'L0_ffn_rn_post2': (1.0, 0.6),
     'L0_ffn_rn_post': (1.0, 0.6),
     'L0_ffn_router_scale': (1.0, 0.6),
     'L0_ffn_per_expert_scale': (1.0, 0.6)}
    factors = {'L0_attn_Wa': 8.0, 'L0_attn_Wb': 8.0, 'L0_attn_Wg': 7.471}
    for name, (base, spread) in spreads.items():
        noise = np.random.default_rng([zlib.crc32(name.encode()), seed]).standard_normal(out[name].shape)
        drawn = base * np.exp(spread * noise) if base else spread * noise
        out[name] = jnp.asarray(drawn.astype(out[name].dtype))
    for name, factor in factors.items():
        out[name] = (out[name] * factor).astype(out[name].dtype)
    return out
```

```python
import concourse.bass as bass
from concourse import mybir
from contextlib import ExitStack

BATCH, SEQ, HID = 2, 2048, 256
TOK = BATCH * SEQ
H, D = 16, 128
P = 128
KT = HID // P
TAPS = 4
C = 32
NCH = SEQ // C
BL = 8
NBL = C // BL
LEAD = C - BL
NT = 512
INNER = 1024
EXPERTS, MI = 8, 128
QD = 4
NG = H // QD

fp32 = mybir.dt.float32
ALU = mybir.AluOpType
ACT = mybir.ActivationFunctionType
AX = mybir.AxisListType


def build(nc, io, scratch):
    with ExitStack() as top:
        with ExitStack() as st:
            xnT = st.enter_context(nc.sbuf_tensor("xnT", [P, KT, TOK], fp32))
            normalise_and_transpose(nc, io, scratch, xnT)
            project_and_convolve(nc, io, scratch, xnT)
        recurrence(nc, io, scratch)
        ffn_and_output(nc, io, scratch)


def normalise_and_transpose(nc, io, scratch, xnT):
    NTILE = TOK // P
    with ExitStack() as st:
        def sb(name, shape):
            return st.enter_context(nc.sbuf_tensor(name, shape, fp32))

        def sem(name):
            return st.enter_context(nc.semaphore(name))

        x_sb = sb("x_sb", [P, NTILE, HID])
        xrT = sb("xrT", [P, KT, TOK])
        ident = sb("identA", [P, P])
        wb = sb("wb", [P, KT, H])
        bb = sb("bb", [H, 1])
        stats = sb("stats", [P, NTILE, 6])
        mv = sb("mv", [P, NTILE, 2])
        rstd = sb("rstd", [P, NTILE])
        shift = sb("shift", [P, NTILE])
        sumsq = sb("sumsq", [P, NTILE])
        rrms = sb("rrms", [P, NTILE])
        squares = sb("squares", [P, HID])
        tiles = sb("tiles", [P, 2, 2, HID])
        beta = sb("beta", [H, TOK])
        pT = st.enter_context(nc.psum_tensor("pT", [P, 2, 2, NT], fp32))
        pB = st.enter_context(nc.psum_tensor("pB", [P, 2, NT], fp32))

        x_in, const_in = sem("x_in"), sem("constA_in")
        stats_step, stats_done = sem("stats_step"), sem("stats_done")
        rstd_done = sem("rstd_done")
        sumsq_done, rrms_done = sem("sumsq_done"), sem("rrms_done")
        xn_ready, xr_ready = sem("xn_ready"), sem("xr_ready")
        tile_free, turned = sem("tile_free"), sem("turned")
        xnT_copied, xrT_copied = sem("xnT_copied"), sem("xrT_copied")
        turn_free = sem("turn_free")
        beta_mm, beta_done, stored = sem("beta_mm"), sem("beta_done"), sem("storedA")
        block = st.enter_context(nc.Block())

        @block.sync
        def _(sp):
            sp.dma_start(x_sb[:], io["x"].rearrange("(n p) c -> p n c", p=P)).then_inc(x_in, 16)
            sp.dma_start(ident[:], io["ident"]).then_inc(const_in, 16)
            sp.dma_start(wb[:], io["WbT"].rearrange("(k p) h -> p k h", p=P)).then_inc(const_in, 16)
            sp.dma_start(bb[:], io["bb"]).then_inc(const_in, 16)
            sp.wait_ge(xnT_copied, NTILE + 1)
            sp.dma_start(scratch["xnT"], xnT[:]).then_inc(stored, 16)
            sp.wait_ge(xrT_copied, NTILE + 1)
            sp.dma_start(scratch["xrT"], xrT[:]).then_inc(stored, 16)
            sp.wait_ge(beta_done, TOK // NT + 1)
            sp.dma_start(scratch["beta"], beta[:]).then_inc(stored, 16)
            sp.wait_ge(stored, 48)

        @block.vector
        def _(dve):
            dve.wait_ge(x_in, 16)
            with dve.Fori(0, NTILE) as n:
                nc.vector.bn_stats(stats[:, bass.ds(n, 1), :], x_sb[:, bass.ds(n, 1), :]).then_inc(stats_step, 1)
            dve.wait_ge(stats_step, NTILE)
            for n in range(NTILE):
                nc.vector.bn_aggr(mv[:, n, :], stats[:, n, :]).then_inc(stats_step, 1)
            dve.wait_ge(stats_step, 2 * NTILE)
            nc.vector.tensor_scalar(rstd[:].unsqueeze(2), mv[:, :, 1:2], 1e-5, None, ALU.add).then_inc(stats_step, 1)
            dve.wait_ge(rstd_done, 1)
            nc.vector.reciprocal(rstd[:], rstd[:]).then_inc(rstd_done, 1)
            dve.wait_ge(rstd_done, 2)
            nc.vector.scalar_tensor_tensor(shift[:], mv[:, :, 0], -1.0, rstd[:], ALU.mult, ALU.mult).then_inc(stats_done, 1)
            dve.wait_ge(sumsq_done, NTILE)
            nc.vector.tensor_scalar(rrms[:], sumsq[:], 1.0 / HID, 1e-6, ALU.mult, ALU.add).then_inc(rrms_done, 1)
            dve.wait_ge(rrms_done, 2)
            nc.vector.reciprocal(rrms[:], rrms[:]).then_inc(rrms_done, 1)
            dve.wait_ge(rrms_done, 3)
            dve.wait_ge(stats_done, 1)

            def copy_xr(n):
                dve.wait_ge(turned, n + 1)
                nc.vector.tensor_copy(xrT[:, :, bass.ds(n * P, P)], pT[:, copy_xr.slot, 1, 0:KT * P].rearrange("p (k t) -> p k t", k=KT)).then_inc(xrT_copied, 1)

            with dve.Fori(0, NTILE // 2) as j:
                for slot in range(2):
                    n = j * 2 + slot
                    dve.wait_ge(tile_free, n + 1)
                    nc.vector.tensor_scalar(tiles[:, slot, 0, :].unsqueeze(1), x_sb[:, bass.ds(n, 1), :], rstd[:, bass.ds(n, 1)], shift[:, bass.ds(n, 1)], ALU.mult, ALU.add).then_inc(xn_ready, 1)
                    dve.wait_ge(xn_ready, n + 1)
                    nc.vector.tensor_scalar(tiles[:, slot, 1, :], tiles[:, slot, 0, :], rrms[:, bass.ds(n, 1)], None, ALU.mult).then_inc(xr_ready, 1)
                    copy_xr.slot = slot
                    copy_xr(n)

        @block.scalar
        def _(act):
            act.wait_ge(stats_step, 2 * NTILE + 1)
            nc.scalar.activation(rstd[:], rstd[:], ACT.Sqrt).then_inc(rstd_done, 1)
            act.wait_ge(stats_done, 1)
            with act.Fori(0, NTILE) as n:
                nc.scalar.activation(squares[:].unsqueeze(1), x_sb[:, bass.ds(n, 1), :], ACT.Square, bias=shift[:, bass.ds(n, 1)], scale=rstd[:, bass.ds(n, 1)],
                                     accum_out=sumsq[:, bass.ds(n, 1)]).then_inc(sumsq_done, 1)
                act.wait_ge(sumsq_done, n + 1)
                act.wait_ge(stats_done, 1)
            act.wait_ge(rrms_done, 1)
            nc.scalar.activation(rrms[:], rrms[:], ACT.Sqrt).then_inc(rrms_done, 1)
            with act.Fori(0, NTILE // 2) as j:
                for slot in range(2):
                    n = j * 2 + slot
                    act.wait_ge(turned, n + 1)
                    nc.scalar.activation(xnT[:, :, bass.ds(n * P, P)], pT[:, slot, 0, 0:KT * P].rearrange("p (k t) -> p k t", k=KT), ACT.Copy).then_inc(xnT_copied, 1)
            act.wait_ge(const_in, 48)
            with act.Fori(0, TOK // NT // 2) as j:
                for slot in range(2):
                    act.wait_ge(beta_mm, j * 2 + slot + 1)
                    nc.scalar.activation(beta[:, bass.ds((j * 2 + slot) * NT, NT)], pB[0:H, slot, :], ACT.Sigmoid, bias=bb[:]).then_inc(beta_done, 1)

        @block.tensor
        def _(pe):
            pe.sem_inc(tile_free, 2)
            for free in (xnT_copied, xrT_copied, beta_done):
                pe.sem_inc(free, 1)
            pe.wait_ge(const_in, 48)
            with pe.Fori(0, NTILE // 2) as j:
                for slot in range(2):
                    n = j * 2 + slot
                    pe.wait_ge(xr_ready, n + 1)
                    if slot == 0:
                        pe.wait_ge(xnT_copied, j * 2 + 1)
                        pe.wait_ge(xrT_copied, j * 2 + 1)
                    for half in range(2):
                        for k in range(KT):
                            last = nc.tensor.transpose(pT[:, slot, half, k * P:(k + 1) * P], tiles[:, slot, half, k * P:(k + 1) * P], ident[:])
                            if half == 0 and k == KT - 1:
                                pass
                    last.then_inc(turned, 1)
                    pe.wait_ge(turned, n + 1)
                    pe.sem_inc(tile_free, 1)
            pe.wait_ge(xnT_copied, NTILE + 1)
            with pe.Fori(0, TOK // NT // 2) as j:
                for slot in range(2):
                    if slot == 0:
                        pe.wait_ge(beta_done, j * 2 + 1)
                    for k in range(KT):
                        last = nc.tensor.matmul(pB[0:H, slot, :], wb[:, k, :], xnT[:, k, bass.ds((j * 2 + slot) * NT, NT)], start=(k == 0), stop=(k == KT - 1))
                    last.then_inc(beta_mm, 1)


def project_and_convolve(nc, io, scratch, xnT):
    QV, KV, VV, AV = range(4)
    ORDER = (KV, QV, VV, AV)
    NCONV = 3 * BATCH
    NUNIT = 4 * BATCH
    NN = SEQ // NT
    with ExitStack() as st:
        def sb(name, shape):
            return st.enter_context(nc.sbuf_tensor(name, shape, fp32))

        def sem(name):
            return st.enter_context(nc.semaphore(name))

        w_stage = sb("w_stage", [P, KT * 4 * P])
        w = sb("w", [P, KT, 4, P])
        par = sb("par", [P, H, 16])
        ba = sb("ba", [P, 1])
        raw = sb("raw", [P, 2, TAPS - 1 + SEQ])
        acc = sb("acc", [P, 2, SEQ])
        kq = sb("kqA", [P, BATCH, (NCH + 1) * C, 2])
        va = sb("vaA", [P, BATCH, NCH, 2, C])
        ps = st.enter_context(nc.psum_tensor("psA", [P, 2, NN, NT], fp32))

        par_in, w_in, w_ready, w_used = sem("par_in"), sem("w_in"), sem("w_ready"), sem("w_used")
        mm, ps_free = sem("mmA"), sem("psA_free")
        pad, raw_ready, raw_free = sem("pad"), sem("raw_ready"), sem("raw_free")
        conv_step, conv_ready, acc_free = sem("conv_step"), sem("conv_ready"), sem("acc_free")
        ba_ready = sem("ba_ready")
        gate_done = sem("gate_done")
        kq_stored, va_stored = sem("kq_stored"), sem("va_stored")
        block = st.enter_context(nc.Block())

        @block.sync
        def _(sp):
            for stored in (kq_stored, va_stored):
                sp.sem_inc(stored, 16)
            sp.dma_start(par[:], io["par"]).then_inc(par_in, 16)
            sp.dma_start(w_stage[:], io["Wqkva"][0]).then_inc(w_in, 16)
            with sp.Fori(0, H) as h:
                sp.wait_ge(w_ready, h + 1)
                nxt = sp.snap(h + 1)
                silus = [sp.snap(h * NCONV + r + 2) for r in range(NCONV)]
                sp.dma_start(w_stage[:], io["Wqkva"][bass.ds(nxt, 1)].rearrange("o p n -> p (o n)")).then_inc(w_in, 16)
                for b in range(BATCH):
                    sp.wait_ge(acc_free, silus[3 * b + 1])
                    sp.dma_start(scratch["kq"][b, :, :, bass.ds(h, 1), :].rearrange("c p h n -> p c (h n)"),
                                 kq[:, b].rearrange("p (c t) e -> p c (t e)", t=C)).then_inc(kq_stored, 16)
                    sp.wait_ge(acc_free, silus[3 * b + 2])
                    sp.dma_start(scratch["va"][b, :, :, bass.ds(h, 1), :].rearrange("c p h n -> p c (h n)"),
                                 va[:, b].rearrange("p c e t -> p c (e t)")).then_inc(va_stored, 16)
            sp.wait_ge(kq_stored, 16 * H * BATCH + 16)
            sp.wait_ge(va_stored, 16 * H * BATCH + 16)
            sp.wait_ge(w_in, 16 * (H + 1))

        @block.gpsimd
        def _(pool):
            nc.gpsimd.memset(raw[:, :, 0:TAPS - 1], 0.0).then_inc(pad, 1)
            nc.gpsimd.memset(kq[:, :, 0:LEAD], 0.0).then_inc(pad, 1)
            nc.gpsimd.memset(kq[:, :, LEAD + SEQ:], 0.0).then_inc(pad, 1)

        @block.tensor
        def _(pe):
            with pe.Fori(0, H) as h:
                pe.wait_ge(w_ready, h + 1)
                for b in range(BATCH):
                    for j, u in enumerate(ORDER):
                        unit = 4 * b + j
                        pe.wait_ge(ps_free, h * NUNIT + unit + 1)
                        for n in range(NN):
                            for k in range(KT):
                                t0 = b * SEQ + n * NT
                                last = nc.tensor.matmul(ps[:, unit % 2, n, :], w[:, k, u, :], xnT[:, k, t0:t0 + NT], start=(k == 0), stop=(k == KT - 1))
                            last.then_inc(mm, 1)
                pe.wait_ge(mm, (h + 1) * NUNIT * NN)
                pe.sem_inc(w_used, 1)

        @block.scalar
        def _(act):
            act.sem_inc(ps_free, 2)
            act.sem_inc(acc_free, 1)
            act.wait_ge(par_in, 16)

            def silu(h, b, v):
                row = 3 * b + v
                act.wait_ge(conv_ready, h * NCONV + row + 1)
                src = acc[:, row % 2, :]
                if v == 0:
                    act.wait_ge(kq_stored, h * 32 + 16)
                if v == 2:
                    act.wait_ge(va_stored, h * 32 + 16)
                if v < 2:
                    dst = kq[:, b, LEAD:LEAD + SEQ, v]
                else:
                    dst, src = va[:, b, :, 0, :], src.rearrange("p (c t) -> p c t", t=C)
                nc.scalar.activation(dst, src, ACT.Silu).then_inc(acc_free, 1)

            with act.Fori(0, H) as h:
                nc.scalar.activation(ba[:], par[:, bass.ds(h, 1), 15], ACT.Copy).then_inc(ba_ready, 1)
                act.wait_ge(ba_ready, h + 1)
                for b in range(BATCH):
                    for j, u in enumerate(ORDER):
                        unit = 4 * b + j
                        if u != AV:
                            row = 3 * b + j
                            act.wait_ge(raw_free, h * NCONV + row + 1)
                            for n in range(NN):
                                act.wait_ge(mm, h * NUNIT * NN + unit * NN + n + 1)
                                nc.scalar.activation(raw[:, row % 2, TAPS - 1 + n * NT:TAPS - 1 + (n + 1) * NT], ps[:, unit % 2, n, :], ACT.Copy).then_inc(raw_ready, 1)
                            act.wait_ge(raw_ready, (h * NCONV + row + 1) * NN)
                            act.sem_inc(ps_free, 1)
                        else:
                            act.wait_ge(va_stored, h * 32 + 16)
                            for n in range(NN):
                                act.wait_ge(mm, h * NUNIT * NN + unit * NN + n + 1)
                                last = nc.scalar.activation(va[:, b, n * NT // C:(n + 1) * NT // C, 1, :], ps[:, unit % 2, n, :].rearrange("p (c t) -> p c t", t=C),
                                                            ACT.Sigmoid, bias=ba[:])
                            last.then_inc(gate_done, 1)
                            act.wait_ge(gate_done, h * BATCH + b + 1)
                            act.sem_inc(ps_free, 1)
                        if j:
                            silu(h, b, j - 1)

        @block.vector
        def _(dve):
            dve.sem_inc(raw_free, 2)
            dve.wait_ge(par_in, 16)
            dve.wait_ge(pad, 3)
            dve.wait_ge(w_in, 16)
            nc.vector.tensor_copy(w[:].rearrange("p k u n -> p (k u n)"), w_stage[:]).then_inc(w_ready, 1)
            with dve.Fori(0, H) as h:
                for b in range(BATCH):
                    for v, u in enumerate(ORDER[:3]):
                        row = 3 * b + v
                        dve.wait_ge(raw_ready, (h * NCONV + row + 1) * NN)
                        if row >= 2:
                            dve.wait_ge(acc_free, h * NCONV + row)
                        else:
                            dve.wait_ge(acc_free, h * NCONV + 1)
                        out = acc[:, row % 2, :]
                        tap = lambda k: par[:, bass.ds(h, 1), TAPS * u + k]
                        nc.vector.tensor_scalar(out, raw[:, row % 2, 0:SEQ], tap(0), par[:, bass.ds(h, 1), 12 + u], ALU.mult, ALU.add).then_inc(conv_step, 1)
                        for k in range(1, TAPS):
                            dve.wait_ge(conv_step, h * (NCONV * 3) + row * 3 + k)
                            ins = nc.vector.scalar_tensor_tensor(out, raw[:, row % 2, k:k + SEQ], tap(k), out, ALU.mult, ALU.add)
                            ins.then_inc(conv_step if k < TAPS - 1 else conv_ready, 1)
                        dve.wait_ge(conv_ready, h * NCONV + row + 1)
                        dve.sem_inc(raw_free, 1)
                        if row == NCONV - 2:
                            dve.wait_ge(w_used, h + 1)
                            dve.wait_ge(w_in, h * 16 + 32)
                            nc.vector.tensor_copy(w[:].rearrange("p k u n -> p (k u n)"), w_stage[:]).then_inc(w_ready, 1)


def act_fills(last=False):
    order = []
    for B in range(NBL):
        for b in range(BATCH):
            order.append(("turn", b, B))
            if B == 0:
                order += [("add", b, Q) for Q in range(QD)]
            if (B, b) in ((0, 1), (1, 0)):
                order += [("state", 1 - b, Q) for Q in range(QD)]
                order += [("base", 1 - b, 0), ("base", 1 - b, 1)]
            if B == 2 and not last:
                order += [("kT", b, 0), ("kg", b, 0)]
    return order


class Count:

    def __init__(self, turn):
        self.turn, self.start, self.n, self.i = turn, 0, 0, None

    def enter(self, i):
        self.start, self.n, self.i = self.start + self.n, 0, i

    def leave(self, turns):
        assert self.n == self.turn, (self.n, self.turn)
        self.start, self.n, self.i = self.start + turns * self.turn, 0, None

    def at(self, back=0):
        v = self.start + self.n - back
        return v if self.i is None else self.i * self.turn + v

    def up(self):
        self.n += 1
        return self.at()


class Link:

    def __init__(self, dve, sem):
        self.dve, self.sem, self.n = dve, sem, 0

    def put(self, ins):
        ins.then_inc(self.sem, 1)
        self.n += 1
        return self.n

    def hold(self, n):
        self.dve.wait_ge(self.sem, n)

    def restart(self):
        self.hold(self.n)
        self.dve.sem_clear(self.sem)
        self.n = 0


def recurrence(nc, io, scratch):
    PAIRS = NCH // 2
    FILLS = act_fills()
    PRE_ORDER = [(what, b, 0) for b in range(BATCH) for what in ("kT", "kg")]
    PRE_FILLS = len(PRE_ORDER)
    ZEROED = 9
    BETA = 1.0 / D
    OSCALE = float(D) ** 0.5
    width = [2 * BL - 1 - 2 * t for t in range(BL)]
    bank_of = [0, 0, 1, 1, 1, 1, 0, 0]
    col_of, used = [], [0, 0]
    for t in range(BL):
        col_of.append(used[bank_of[t]])
        used[bank_of[t]] += H * width[t]
    assert max(used) <= NT

    with ExitStack() as st:
        def sb(name, shape):
            return st.enter_context(nc.sbuf_tensor(name, shape, fp32))

        def pb(name, shape):
            return st.enter_context(nc.psum_tensor(name, shape, fp32))

        def sem(name):
            return st.enter_context(nc.semaphore(name))

        def sems(name):
            return [sem(f"{name}{b}") for b in range(BATCH)]

        kq = sb("kq", [P, 2, BATCH, H, C, 2])
        va = sb("va", [P, 2, BATCH, H, 2, C])
        own = sb("own", [P, 2, BATCH, NBL, H, 2 * BL])
        kr = sb("kr", [P, BATCH, H, C])
        kown = sb("kown", [P, BATCH, NBL, H, BL])
        kg = sb("kg", [P, 2, BATCH, NG, QD, 2 * C])
        kT = sb("kT", [P, 2, BATCH, NG, D])
        S = sb("S", [P, BATCH, H, D])
        ST = sb("ST", [P, BATCH, H, D])
        base = sb("base", [P, BATCH, H, 2 * C])
        U = sb("U", [P, BATCH, QD, NT])
        X = sb("X", [P, BATCH, 2, H, 2 * BL])
        Y = sb("Y", [P, BATCH, H * (2 * BL - 1)])
        E = sb("E", [P, BATCH, H, C])
        ET = sb("ET", [P, BATCH, NG, D])
        dsuf = sb("dsuf", [P, 2, BATCH, H, NBL, BL])
        dblk = sb("dblk", [P, 2, BATCH, H, NBL])
        dcum = sb("dcum", [P, 2, BATCH, H, NBL])
        o = sb("o", [P, 2, BATCH, H, C])
        sel = sb("sel", [P, BL, P])
        ident = sb("identB", [P, P])
        mask = sb("mask", [P, H, 2 * BL])
        bown = sb("bown", [P, BATCH, SEQ // BL])
        b32 = sb("b32", [P, BATCH, NG, NCH])
        bt_own = sb("bt_own", [P, BATCH, 2, H, BL])
        bt_32 = sb("bt_32", [NCH, BATCH, H, C])
        unit = sb("unit", [P, 2])
        b32c = sb("b32c", [P, BATCH, NG])
        psel = pb("psel", [P, BATCH, 2, NT])
        pact = pb("pact", [P, 2, NT])
        phist = pb("phist", [P, NT])
        pown = pb("pown", [P, NT])

        consts_in, beta_in, zeroed = sem("consts_in"), sem("beta_in"), sem("zeroed")
        beta_turned, beta_scaled = sem("beta_turned"), sem("beta_scaled")
        kq_in, va_in = [sems("kq_in_s0_"), sems("kq_in_s1_")], [sems("va_in_s0_"), sems("va_in_s1_")]
        act_fill, act_evac = sem("act_fill"), sem("act_evac")
        own_fill, own_evac = sem("own_fill"), sem("own_evac")
        hist_fill, hist_evac = sem("hist_fill"), sem("hist_evac")
        sel_ready, sel_used = sems("sel_ready"), sems("sel_used")
        e_ready, x_done = sems("e_ready"), sems("x_done")
        decay_step, decay_ready, s_added = sem("decay_step"), sems("decay_ready"), sems("s_added")
        o_copied, o_stored, chain = sems("o_copied"), [sems("o_stored_s0_"), sems("o_stored_s1_")], sem("chain")
        b32c_ready, k_laid = sem("b32c_ready"), sems("k_laid")
        block = st.enter_context(nc.Block())

        def evacs(c, tag, b, n):
            return c * len(FILLS) + PRE_FILLS + FILLS.index((tag, b, n)) + 1

        @block.sync
        def _(sp):
            def load(c, slot, b):
                sp.dma_start(kq[:, slot, b].rearrange("p h t e -> p (h t e)"), scratch["kq"][b, bass.ds(c + 1, 1)].rearrange("c p h n -> p (c h n)")).then_inc(kq_in[slot][b], 16)

            def load_va(c, slot, b):
                sp.dma_start(va[:, slot, b].rearrange("p h e t -> p (h e t)"), scratch["va"][b, bass.ds(c, 1)].rearrange("c p h n -> p (c h n)")).then_inc(va_in[slot][b], 16)

            sp.dma_start(ident[:], io["ident"]).then_inc(consts_in, 16)
            sp.dma_start(sel[:], io["sel"]).then_inc(consts_in, 16)
            sp.dma_start(mask[:], io["mask"]).then_inc(consts_in, 16)
            for b in range(BATCH):
                load(-1, 1, b)
                load(0, 0, b)
                load_va(0, 0, b)
            for b in range(BATCH):
                row = scratch["beta"][:, b * SEQ:(b + 1) * SEQ]
                for half in range(2):
                    part = row[:, half * P * BL:(half + 1) * P * BL]
                    sp.dma_start(bt_own[:, b, half], part.rearrange("h (n s) -> n h s", s=BL)).then_inc(beta_in, 16)
                sp.dma_start(bt_32[:, b], row.rearrange("h (c s) -> c h s", s=C)).then_inc(beta_in, 16)
            for b in range(BATCH):
                load_va(1, 1, b)
            sp.wait_ge(own_fill, BATCH)
            for b in range(BATCH):
                load(1, 1, b)

            def store(c, slot, b):
                sp.dma_start(scratch["o"][b, bass.ds(c, 1)].rearrange("c p h n -> p (c h n)"), o[:, slot, b].rearrange("p h t -> p (h t)")).then_inc(o_stored[slot][b], 16)

            def chunk(c, slot, more):
                for b in range(BATCH):
                    if more:
                        sp.wait_ge(act_fill, evacs(c, "base", b, 1))
                        load(c + 2, slot, b)
                for b in range(BATCH):
                    if more:
                        sp.wait_ge(x_done[b], c * NBL + NBL)
                        load_va(c + 2, slot, b)
                    sp.wait_ge(o_copied[b], c * NBL + NBL + 2)
                    store(c, slot, b)

            for b in range(BATCH):
                for slot in range(2):
                    sp.sem_inc(o_stored[slot][b], 16)
            with sp.Fori(0, PAIRS - 1) as i:
                chunk(i * 2, 0, True)
                chunk(i * 2 + 1, 1, True)
            chunk(NCH - 2, 0, False)
            chunk(NCH - 1, 1, False)
            for b in range(BATCH):
                for slot in range(2):
                    sp.wait_ge(o_stored[slot][b], PAIRS * 16 + 16)

        @block.gpsimd
        def _(pool):
            PER = BL + NBL

            for t in (S, E, kT, kg, base, dcum):
                nc.gpsimd.memset(t[:], 0.0).then_inc(zeroed, 1)
            nc.gpsimd.memset(dsuf[:].rearrange("p s b h n t -> p (s b h n) t")[:, :, BL - 1], 1.0).then_inc(zeroed, 1)
            nc.gpsimd.memset(unit[:, 0:1], 1.0).then_inc(zeroed, 1)
            nc.gpsimd.memset(unit[:, 1:2], OSCALE).then_inc(zeroed, 1)
            pool.wait_ge(zeroed, ZEROED)
            for b in range(BATCH):
                pool.sem_inc(o_copied[b], 2)

            def decays(c, slot, b, loads):
                k = (c * BATCH + b) * (PER - 1)
                pool.wait_ge(va_in[slot][b], loads * 16)
                a = va[:, slot, b, :, 1, :].rearrange("p h (n s) -> p h n s", s=BL)
                f = dsuf[:, slot, b]
                chained = [(f[:, :, :, s], f[:, :, :, s + 1], a[:, :, :, s + 1]) for s in range(BL - 2, -1, -1)]
                chained += [(dblk[:, slot, b], f[:, :, :, 0], a[:, :, :, 0]), (dcum[:, slot, b, :, 0], dblk[:, slot, b, :, 0], f[:, :, 0, BL - 1])]
                chained += [(dcum[:, slot, b, :, n], dcum[:, slot, b, :, n - 1], dblk[:, slot, b, :, n]) for n in range(1, NBL)]
                for n, (out, x, y) in enumerate(chained):
                    if n:
                        pool.wait_ge(decay_step, k + n)
                    nc.gpsimd.tensor_tensor(out, x, y, ALU.mult).then_inc(decay_step if n < PER - 1 else decay_ready[b], 1)
                assert len(chained) == PER

            def lay_keys(slot, b, loads):
                pool.wait_ge(kq_in[slot][b], loads * 16)
                one = unit[:, 0:1].unsqueeze(2)
                nc.gpsimd.tensor_tensor(kr[:, b, :, 0:BL], kq[:, 1 - slot, b, :, LEAD:C, 0], one.to_broadcast([P, H, BL]), ALU.mult)
                nc.gpsimd.tensor_tensor(kr[:, b, :, BL:C], kq[:, slot, b, :, 0:LEAD, 0], one.to_broadcast([P, H, LEAD]), ALU.mult)
                for B in range(NBL):
                    src = kq[:, slot, b, :, (B - 1) * BL:B * BL, 0] if B else kq[:, 1 - slot, b, :, LEAD:C, 0]
                    last = nc.gpsimd.tensor_tensor(kown[:, b, B], src, one.to_broadcast([P, H, BL]), ALU.mult)
                last.then_inc(k_laid[b], 1)

            def add_state(c, b):
                for Q in range(QD):
                    pool.wait_ge(act_evac, evacs(c, "add", b, Q))
                    part = S[:, b].rearrange("p (g q) n -> p q g n", q=QD)[:, Q]
                    nc.gpsimd.tensor_tensor(part, part, U[:, b, Q].rearrange("p (g n) -> p g n", g=NG), ALU.add).then_inc(s_added[b], 1)

            def chunk(c, slot, last, turn):
                for B in range(NBL):
                    if B == 0:
                        add_state(c, 0)
                        if not last:
                            pool.wait_ge(own_fill, c * BATCH * NBL + BATCH * NBL)
                            for b in range(BATCH):
                                lay_keys(1 - slot, b, turn + 2)
                        add_state(c, 1)
                    for b in range(BATCH):
                        if B == 1 and not last:
                            pool.wait_ge(decay_ready[b], c + 1)
                            pool.wait_ge(act_evac, evacs(c, "state", b, QD - 1))
                            nc.gpsimd.tensor_tensor(S[:, b], S[:, b], dcum[:, slot, b, :, NBL - 1:NBL].to_broadcast([P, H, D]), ALU.mult)
                        if B == 2 and not last:
                            decays(c + 1, 1 - slot, b, turn + slot + 1)
                        if B == 0:
                            pool.wait_ge(o_stored[slot][b], turn * 16 + 16)
                        pool.wait_ge(x_done[b], c * NBL + B + 1)
                        nc.gpsimd.tensor_tensor(o[:, slot, b, :, B * BL:(B + 1) * BL], X[:, b, B % 2].rearrange("p h (t e) -> p h t e", e=2)[:, :, :, 1],
                                                unit[:, 1:2].unsqueeze(2).to_broadcast([P, H, BL]), ALU.mult).then_inc(o_copied[b], 1)

            for b in range(BATCH):
                pool.wait_ge(kq_in[1][b], 16)
                lay_keys(0, b, 1)
                decays(0, 0, b, 1)
            with pool.Fori(0, PAIRS - 1) as i:
                chunk(i * 2, 0, False, i)
                chunk(i * 2 + 1, 1, False, i)
            chunk(NCH - 2, 0, False, PAIRS - 1)
            chunk(NCH - 1, 1, True, PAIRS - 1)

        @block.scalar
        def _(act):
            def betas(c):
                nc.scalar.activation(b32c[:].unsqueeze(3), b32[:, :, :, bass.ds(c, 1)], ACT.Copy).then_inc(b32c_ready, 1)
                act.wait_ge(b32c_ready, c + 1)

            def evac(c, tag, b, n, bank, slot):
                src = pact[:, bank]
                if tag == "base":
                    if n == 0:
                        act.wait_ge(hist_evac, c * BATCH * NBL + b + 2)
                    last = nc.scalar.activation(base[:, b, n * H // 2:(n + 1) * H // 2].rearrange("p h n -> p (h n)"), src, ACT.Copy)
                elif tag == "add":
                    last = nc.scalar.activation(U[:, b, n], src, ACT.Copy)
                elif tag == "turn":
                    last = nc.scalar.activation(ET[:, b].rearrange("p g n -> p (g n)"), src, ACT.Copy)
                elif tag == "state":
                    last = nc.scalar.activation(ST[:, b].rearrange("p (g q) n -> p q g n", q=QD)[:, n], src.rearrange("p (g n) -> p g n", g=NG), ACT.Copy)
                elif tag == "kT":
                    for g in range(NG):
                        last = nc.scalar.activation(kT[:, slot, b, g], src[:, g * D:(g + 1) * D], ACT.Copy, scale=b32c[:, b, g:g + 1])
                else:
                    for g in range(NG):
                        for Q in range(QD):
                            rows = slice(Q * C, (Q + 1) * C)
                            last = nc.scalar.activation(kg[rows, slot, b, g, Q], src[rows, g * 2 * C:(g + 1) * 2 * C], ACT.Copy, scale=b32c[rows, b, g:g + 1])
                last.then_inc(act_evac, 1)

            def chunk(c, slot, last):
                for n, (tag, b, k) in enumerate(act_fills(last)):
                    act.wait_ge(act_fill, c * len(FILLS) + PRE_FILLS + n + 1)
                    if (tag, b) == ("kT", 0):
                        betas(c + 1)
                    evac(c, tag, b, k, (PRE_FILLS + n) % 2, 1 - slot)

            act.wait_ge(beta_turned, 1)
            nc.scalar.activation(bown[:].rearrange("p b n -> p (b n)"), pact[:, 0], ACT.Copy, scale=BETA).then_inc(beta_scaled, 1)
            nc.scalar.activation(b32[:].rearrange("p b g c -> p (b g c)"), pact[:, 1], ACT.Copy, scale=BETA).then_inc(beta_scaled, 1)
            act.wait_ge(beta_scaled, 2)
            act.wait_ge(zeroed, ZEROED)
            betas(0)
            for n, (tag, b, k) in enumerate(PRE_ORDER):
                act.wait_ge(act_fill, n + 1)
                evac(0, tag, b, k, n % 2, 0)
            with act.Fori(0, PAIRS - 1) as i:
                chunk(i * 2, 0, False)
                chunk(i * 2 + 1, 1, False)
            chunk(NCH - 2, 0, False)
            chunk(NCH - 1, 1, True)

        @block.tensor
        def _(pe):
            owns, hists = Count(2 * BATCH * NBL), Count(2 * BATCH * NBL)
            fills = Count(2 * len(FILLS))

            def act_bank():
                bank = (fills.start + fills.n) % 2
                if fills.i is not None or fills.start + fills.n >= 2:
                    pe.wait_ge(act_evac, fills.at(1))
                return pact[:, bank]

            def filled(last):
                last.then_inc(act_fill, 1)
                fills.up()

            def turn_E(b):
                dst = act_bank()
                for g in range(NG):
                    last = nc.tensor.transpose(dst[:, g * P:(g + 1) * P], E[:, b, g * QD:(g + 1) * QD].rearrange("p h s -> p (h s)"), ident[:])
                filled(last)
                return fills.at()

            def bases(slot, b):
                pe.wait_ge(act_evac, fills.at())
                for half in range(2):
                    dst = act_bank()
                    for h in range(H // 2):
                        hh = half * H // 2 + h
                        last = nc.tensor.matmul(dst[:, h * 2 * C:(h + 1) * 2 * C], ST[:, b, hh], kq[:, slot, b, hh].rearrange("p t e -> p (t e)"), start=True, stop=True)
                    filled(last)

            def keys(slot, b):
                dst = act_bank()
                for g in range(NG):
                    last = nc.tensor.transpose(dst[:, g * P:(g + 1) * P], kr[:, b, g * QD:(g + 1) * QD].rearrange("p h t -> p (h t)"), ident[:])
                filled(last)
                dst = act_bank()
                for g in range(NG):
                    for Q in range(QD):
                        h = g * QD + Q
                        last = nc.tensor.matmul(dst[Q * C:(Q + 1) * C, g * 2 * C:(g + 1) * 2 * C], kr[:, b, h], kq[:, slot, b, h].rearrange("p t e -> p (t e)"),
                                                start=True, stop=True, tile_position=(0, Q * C))
                filled(last)

            def own_bank():
                if owns.i is not None or owns.start + owns.n:
                    pe.wait_ge(own_evac, owns.at())
                return pown

            def own_block(slot, b, B):
                dst = own_bank()
                pairs = kq[:, slot, b, :, (B - 1) * BL:B * BL] if B else kq[:, 1 - slot, b, :, LEAD:C]
                nc.tensor.matmul(dst[:, 0:H * 2 * BL], kown[:, b, B].rearrange("p h s -> p (h s)"), pairs.rearrange("p h t e -> p h (t e)"),
                                 start=True, stop=True).then_inc(own_fill, 1)
                owns.up()

            def sel_block(c, slot, b, B):
                for bank in (1, 0):
                    pe.wait_ge(sel_used[b], (c * NBL + B) * 2 + (1 if bank else 2))
                    for t in range(BL):
                        if bank_of[t] == bank:
                            last = nc.tensor.matmul(psel[:, b, bank, col_of[t]:col_of[t] + H * width[t]], sel[:, t], own[:, slot, b, B, :, 2 * t + 1:2 * BL], start=True, stop=True)
                    last.then_inc(sel_ready[b], 1)

            def history(slot, b, B, turned):
                pe.wait_ge(act_evac, turned)
                pe.wait_ge(hist_evac, hists.at() + 1)
                slot, n = (slot, B - 1) if B else (1 - slot, NBL - 1)
                for g in range(NG):
                    last = nc.tensor.matmul(phist[:, g * QD * 2 * BL:(g + 1) * QD * 2 * BL], ET[:, b, g], kg[:, slot, b, g, :, n * 2 * BL:(n + 1) * 2 * BL], start=True, stop=True)
                last.then_inc(hist_fill, 1)
                hists.up()

            def adds(slot, b):
                for Q in range(QD):
                    dst = act_bank()
                    rows = slice(Q * C, (Q + 1) * C)
                    for g in range(NG):
                        last = nc.tensor.matmul(dst[:, g * D:(g + 1) * D], ET[rows, b, g], kT[rows, 1 - slot, b, g], start=True, stop=True, tile_position=(Q * C, 0))
                    filled(last)

            def state_T(c, b):
                for Q in range(QD):
                    pe.wait_ge(s_added[b], c * QD + Q + 1)
                    dst = act_bank()
                    for g in range(NG):
                        last = nc.tensor.transpose(dst[:, g * P:(g + 1) * P], S[:, b, g * QD + Q], ident[:])
                    filled(last)

            def chunk(c, slot, last, next_loads):
                for B in range(NBL):
                    for b in range(BATCH):
                        pe.wait_ge(e_ready[b], c * NBL + B + 1)
                        turned = turn_E(b)
                        sel_block(c, slot, b, B)
                        history(slot, b, B, turned)
                        if B == 0:
                            adds(slot, b)
                        if not last:
                            if B == 0:
                                pe.wait_ge(kq_in[1 - slot][b], next_loads * 16)
                                pe.wait_ge(k_laid[b], c + 2)
                            own_block(1 - slot, b, B)
                        if (B, b) in ((0, 1), (1, 0)):
                            state_T(c, 1 - b)
                            bases(slot, 1 - b)
                        if B == 2 and not last:
                            keys(1 - slot, b)

            pe.wait_ge(consts_in, 48)
            pe.wait_ge(beta_in, 16 * 3 * BATCH)
            for b in range(BATCH):
                for half in range(2):
                    at = (b * 2 + half) * P
                    nc.tensor.transpose(pact[:, 0, at:at + P], bt_own[:, b, half].rearrange("n h s -> n (h s)"), ident[:])
                for g in range(NG):
                    at = (b * NG + g) * NCH
                    last = nc.tensor.transpose(pact[:, 1, at:at + NCH], bt_32[:, b, g * QD:(g + 1) * QD].rearrange("c h s -> c (h s)"), ident[0:NCH, 0:NCH])
            last.then_inc(beta_turned, 1)
            pe.wait_ge(beta_scaled, 2)
            pe.wait_ge(zeroed, ZEROED)
            for b in range(BATCH):
                pe.wait_ge(kq_in[0][b], 16)
                pe.wait_ge(kq_in[1][b], 16)
                pe.wait_ge(k_laid[b], 1)
                keys(0, b)
            for B in range(NBL):
                for b in range(BATCH):
                    own_block(0, b, B)
            pe.wait_ge(own_evac, BATCH * NBL)
            assert fills.n == PRE_FILLS
            with pe.Fori(0, PAIRS - 1) as i:
                for k in (owns, hists, fills):
                    k.enter(i)
                chunk(i * 2, 0, False, i + 2)
                chunk(i * 2 + 1, 1, False, i + 2)
            for k in (owns, hists, fills):
                k.leave(PAIRS - 1)
            chunk(NCH - 2, 0, False, PAIRS + 1)
            chunk(NCH - 1, 1, True, 0)

        @block.vector
        def _(dve):
            owns, hists = Count(2 * BATCH * NBL), Count(2 * BATCH * NBL)
            link = Link(dve, chain)

            def own_out(col, slot, b, B):
                dve.wait_ge(own_fill, owns.up())
                nc.vector.scalar_tensor_tensor(own[:, slot, b, B], pown[:, 0:H * 2 * BL].rearrange("p (h n) -> p h n", h=H), bown[:, b, bass.ds(col, 1)] if not isinstance(col, int) else bown[:, b, col:col + 1],
                                               mask[:], ALU.mult, ALU.mult).then_inc(own_evac, 1)

            def block_steps(c, slot, b, B):
                Xb, v, a = X[:, b, B % 2], va[:, slot, b, :, 0], va[:, slot, b, :, 1]
                dve.wait_ge(o_copied[b], c * NBL + B + 1)
                from_slot, n = (slot, B - 1) if B else (1 - slot, NBL - 1)
                start = base[:, b, :, n * 2 * BL:(n + 1) * 2 * BL]
                if B == 1:
                    dve.wait_ge(act_evac, evacs(c, "base", b, 1))
                x_now = link.put(nc.vector.tensor_tensor(Xb, start, dcum[:, from_slot, b, :, n:n + 1].to_broadcast([P, H, 2 * BL]), ALU.mult))
                filled = hists.up()
                dve.wait_ge(hist_fill, filled)
                if B == 0:
                    link.hold(link.put(nc.vector.memset(E[:, b], 0.0)))
                link.hold(x_now)
                nc.vector.tensor_tensor(Xb, Xb, phist[:, 0:H * 2 * BL].rearrange("p (h n) -> p h n", h=H), ALU.add).then_inc(hist_evac, 1)
                dve.wait_ge(hist_evac, filled + 1)
                dve.wait_ge(sel_ready[b], (c * NBL + B) * 2 + 2)
                for t in range(BL):
                    s, w = B * BL + t, width[t]
                    if t:
                        link.hold(x_now)
                    e = E[:, b, :, s:s + 1]
                    e_now = link.put(nc.vector.tensor_tensor(e, v[:, :, s:s + 1], Xb[:, :, 2 * t:2 * t + 1], ALU.subtract))
                    rest = Xb[:, :, 2 * t + 1:2 * BL]
                    xa_now = link.put(nc.vector.tensor_tensor(rest, rest, a[:, :, s:s + 1].to_broadcast([P, H, w]), ALU.mult))
                    y = Y[:, b, 0:H * w].rearrange("p (h n) -> p h n", h=H)
                    kgt = psel[:, b, bank_of[t], col_of[t]:col_of[t] + H * w].rearrange("p (h n) -> p h n", h=H)
                    link.hold(e_now)
                    ins = nc.vector.tensor_tensor(y, kgt, e.to_broadcast([P, H, w]), ALU.mult)
                    if t in (5, 7):
                        ins.then_inc(sel_used[b], 1)
                        dve.wait_ge(sel_used[b], (c * NBL + B) * 2 + (3 if t == 5 else 4))
                        link.hold(xa_now)
                    else:
                        link.hold(link.put(ins))
                    ins = nc.vector.tensor_tensor(rest, rest, y, ALU.add)
                    if t < BL - 1:
                        x_now = link.put(ins)
                    else:
                        ins.then_inc(x_done[b], 1)
                mine = E[:, b, :, B * BL:(B + 1) * BL]
                ins = nc.vector.tensor_tensor(mine, mine, dsuf[:, slot, b, :, B], ALU.mult)
                if B:
                    past = E[:, b, :, 0:B * BL]
                    ins = nc.vector.tensor_tensor(past, past, dblk[:, slot, b, :, B:B + 1].to_broadcast([P, H, B * BL]), ALU.mult)
                ins.then_inc(e_ready[b], 1)
                dve.wait_ge(e_ready[b], c * NBL + B + 2)

            def chunk(c, slot, last, loads):
                for B in range(NBL):
                    for b in range(BATCH):
                        if B == 0:
                            dve.wait_ge(va_in[slot][b], loads * 16)
                            dve.wait_ge(decay_ready[b], c + 1)
                        block_steps(c, slot, b, B)
                        if not last:
                            own_out((c + 1) * NBL + B, 1 - slot, b, B)
                link.restart()

            for b in range(BATCH):
                dve.sem_inc(sel_used[b], 2)
                dve.sem_inc(e_ready[b], 1)
            dve.sem_inc(hist_evac, 1)
            dve.wait_ge(consts_in, 48)
            dve.wait_ge(beta_scaled, 2)
            dve.wait_ge(zeroed, ZEROED)
            for B in range(NBL):
                for b in range(BATCH):
                    own_out(B, 0, b, B)
            with dve.Fori(0, PAIRS - 1) as i:
                for k in (owns, hists):
                    k.enter(i)
                chunk(i * 2, 0, False, i + 1)
                chunk(i * 2 + 1, 1, False, i + 1)
            for k in (owns, hists):
                k.leave(PAIRS - 1)
            chunk(NCH - 2, 0, False, PAIRS)
            chunk(NCH - 1, 1, True, PAIRS)


def ffn_and_output(nc, io, scratch):
    TILES = TOK // NT
    SUB = NT // P
    CT = NT // C
    HIDDEN = INNER // P + EXPERTS
    ND = INNER // P
    OSLOTS = 4
    with ExitStack() as st:
        def sb(name, shape):
            return st.enter_context(nc.sbuf_tensor(name, shape, fp32))

        def pb(name, shape):
            return st.enter_context(nc.psum_tensor(name, shape, fp32))

        def sem(name):
            return st.enter_context(nc.semaphore(name))

        w_g = sb("w_g", [P, KT, HIDDEN, P])
        w_u = sb("w_u", [P, KT, HIDDEN, P])
        w_d = sb("w_d", [P, HIDDEN, HID])
        w_r = sb("w_r", [P, KT, EXPERTS])
        wg_a = sb("wg_a", [P, KT, H * D])
        w_o = sb("w_o", [P, H, HID])
        pre = sb("pre", [P, KT, 3])
        post = sb("post", [P, 3, HID])
        pes = sb("pes", [P, EXPERTS])
        rank = sb("rank", [P, EXPERTS])
        ln = sb("ln", [P, 2])
        eps = sb("eps", [P, 1])
        cen = sb("cen", [P, P])
        avg = sb("avg", [P, P])
        xr = sb("xr", [P, 2, KT, NT])
        xn = sb("xn", [P, 2, KT, NT])
        hg = sb("hg", [P, 2, NT])
        hid = sb("hid", [P, HIDDEN, NT])
        gate = sb("gate", [P, H, NT])
        o_c = sb("o_c", [P, OSLOTS, NT])
        sq = sb("sq", [P, 2, NT])
        sd = sb("sd", [P, 2, NT])
        cn = sb("cn", [P, 2, NT])
        og = gate
        lg = sb("lg", [P, 6, SUB, EXPERTS])
        rs = sb("rs", [P, 8, SUB])
        aff = sb("aff", [P, SUB, EXPERTS])
        x_t = sb("x_t", [P, SUB, HID])
        dn = sb("dn", [P, SUB, HID])
        mo = sb("mo", [P, SUB, HID])
        s_t = sb("s_t", [P, SUB, HID])
        junk2 = sb("junk2", [P, 2, HID])
        ss = sb("ss", [P, 3, SUB])
        rr = sb("rr", [P, 3, SUB])
        pA = pb("pA", [P, 2, NT])
        pU = pb("pU", [P, 2, NT])
        pV = pb("pV", [P, NT])
        pS = pb("pS", [P, NT])
        pE = pb("pE", [P, 2, NT])

        w_in, w_scaled, eps_set = sem("wC_in"), sem("w_scaled"), sem("eps_set")
        xt_in, x_in = [sem("xt_in0"), sem("xt_in1")], sem("xC_in")
        o_in = [sem(f"o_in{k}") for k in range(OSLOTS)]
        a_fill, a_read = sem("a_fill"), sem("a_read")
        u_fill, u_read = sem("u_fill"), sem("u_read")
        v_fill, v_read = sem("v_fill"), sem("v_read")
        s_fill, s_read = sem("s_fill"), sem("s_read")
        e_fill, e_read = sem("e_fill"), sem("e_read")
        sq_done, og_done = sem("sq_done"), sem("og_done")
        cn_ready = sem("cn_ready")
        exp_in, exp_done = sem("exp_in"), sem("exp_done")
        mo_done, ms_ready, rms_done = sem("mo_done"), sem("ms_ready"), sem("rms_done")
        ssy_done, y_ready, y_done = sem("ssy_done"), sem("y_ready"), sem("y_done")
        out_ready, out_stored, chain, act_chain = sem("out_ready"), sem("out_stored"), sem("chainC"), sem("act_chain")
        block = st.enter_context(nc.Block())
        NW = 16 * 18

        @block.sync
        def _(sp):
            wide = lambda name: io[name].rearrange("(k p) n -> p k n", p=P)
            sp.dma_start(w_g[:, :, 0:ND].rearrange("p k n m -> p k (n m)"), wide("w_gate")).then_inc(w_in, 16)
            sp.dma_start(w_u[:, :, 0:ND].rearrange("p k n m -> p k (n m)"), wide("w_up")).then_inc(w_in, 16)
            for k in range(KT):
                sp.dma_start(w_g[:, k, ND:], io["we_gate"][:, k * P:(k + 1) * P, :].rearrange("e p m -> p e m")).then_inc(w_in, 16)
                sp.dma_start(w_u[:, k, ND:], io["we_up"][:, k * P:(k + 1) * P, :].rearrange("e p m -> p e m")).then_inc(w_in, 16)
            sp.dma_start(w_d[:, 0:ND], io["w_down"].rearrange("(n p) c -> p n c", p=P)).then_inc(w_in, 16)
            sp.dma_start(w_d[:, ND:], io["we_down"].rearrange("e p c -> p e c")).then_inc(w_in, 16)
            sp.dma_start(w_r[:], wide("router_w")).then_inc(w_in, 16)
            sp.dma_start(wg_a[:], wide("WgT")).then_inc(w_in, 16)
            sp.dma_start(w_o[:], io["WoT"].rearrange("(h p) c -> p h c", p=P)).then_inc(w_in, 16)
            sp.dma_start(pre[:], io["pre"].rearrange("(k p) n -> p k n", p=P)).then_inc(w_in, 16)
            sp.dma_start(post[:].rearrange("p n c -> p (n c)"), io["post"].partition_broadcast(P)).then_inc(w_in, 16)
            sp.dma_start(pes[:], io["pes"].partition_broadcast(P)).then_inc(w_in, 16)
            for t, name in ((rank, "rank"), (ln, "ln"), (cen, "cen"), (avg, "avg")):
                sp.dma_start(t[:], io[name]).then_inc(w_in, 16)

            def tile(j, slot, n):
                at = n * NT
                sp.dma_start(xr[:, slot], scratch["xrT"][:, :, bass.ds(at, NT)]).then_inc(xt_in[slot], 16)
                sp.dma_start(xn[:, slot], scratch["xnT"][:, :, bass.ds(at, NT)]).then_inc(xt_in[slot], 16)

            def chunk_load(n, cc, free):
                if free is not None:
                    sp.wait_ge(u_fill, free)
                sp.dma_start(o_c[:, cc % OSLOTS], scratch["o"][:].rearrange("b c p h t -> (b c) p (h t)")[bass.ds(n * CT + cc, 1)].rearrange("c p n -> p (c n)")).then_inc(o_in[cc % OSLOTS], 16)

            sp.sem_inc(out_stored, 16)
            with sp.Fori(0, TILES // 2) as j:
                for slot in range(2):
                    n = j * 2 + slot
                    tile(j, slot, n)
                    if slot == 0:
                        sp.wait_ge(out_stored, j * 32 + 16)
                    else:
                        sp.wait_ge(out_stored, j * 32 + 32)
                    sp.dma_start(x_t[:], io["x"].rearrange("(n s p) c -> n p s c", p=P, s=SUB)[bass.ds(n, 1)].rearrange("n p s c -> p (n s) c")).then_inc(x_in, 16)
                    for cc in range(CT):
                        chunk_load(n, cc, n * (HIDDEN + CT) + HIDDEN + cc - OSLOTS + 1 if cc >= OSLOTS else n * (HIDDEN + CT) + 1)
                    sp.wait_ge(out_ready, n + 1)
                    sp.dma_start(io["out"].rearrange("(n s p) c -> n p s c", p=P, s=SUB)[bass.ds(n, 1)].rearrange("n p s c -> p (n s) c"), s_t[:]).then_inc(out_stored, 16)
            sp.wait_ge(out_stored, TILES * 16 + 16)

        @block.gpsimd
        def _(pool):
            nc.gpsimd.memset(eps[:], 1e-5).then_inc(eps_set, 1)
            pool.sem_inc(og_done, 2)
            with pool.Fori(0, TILES) as n:
                for cc in range(CT):
                    pool.wait_ge(cn_ready, n * CT + cc + 1)
                    nc.gpsimd.tensor_tensor(og[:, :, cc * C:(cc + 1) * C], cn[:, cc % 2].rearrange("p (h t) -> p h t", h=H), gate[:, :, cc * C:(cc + 1) * C], ALU.mult).then_inc(og_done, 1)

        @block.tensor
        def _(pe):
            A, U, V, SS, EE = Count(2 * (HIDDEN + H)), Count(2 * (HIDDEN + CT)), Count(2 * (CT + SUB)), Count(2 * SUB), Count(2 * (1 + SUB * EXPERTS // 2))
            counts = (A, U, V, SS, EE)

            def tile(j, slot):
                n = j * 2 + slot
                pe.wait_ge(xt_in[slot], j * 32 + 32)
                pe.wait_ge(e_read, EE.at(0) + 1)
                for s in range(SUB):
                    for k in range(KT):
                        last = nc.tensor.matmul(pE[:, 0, s * EXPERTS:(s + 1) * EXPERTS], xr[:, slot, k, s * P:(s + 1) * P], w_r[:, k], start=(k == 0), stop=(k == KT - 1))
                last.then_inc(e_fill, 1)
                EE.up()
                for m in range(HIDDEN):
                    pe.wait_ge(a_read, A.at() + 1)
                    for k in range(KT):
                        last = nc.tensor.matmul(pA[:, m % 2], w_g[:, k, m], xr[:, slot, k], start=(k == 0), stop=(k == KT - 1))
                    last.then_inc(a_fill, 1)
                    A.up()
                    pe.wait_ge(u_read, U.at() + 1)
                    for k in range(KT):
                        last = nc.tensor.matmul(pU[:, m % 2], w_u[:, k, m], xr[:, slot, k], start=(k == 0), stop=(k == KT - 1))
                    last.then_inc(u_fill, 1)
                    U.up()
                for h in range(H):
                    pe.wait_ge(a_read, A.at() + 1)
                    for k in range(KT):
                        last = nc.tensor.matmul(pA[:, h % 2], wg_a[:, k, h * D:(h + 1) * D], xn[:, slot, k], start=(k == 0), stop=(k == KT - 1))
                    last.then_inc(a_fill, 1)
                    A.up()

                def variance(cc):
                    pe.wait_ge(sq_done, n * CT + cc + 1)
                    pe.wait_ge(v_read, V.at() + 1)
                    nc.tensor.matmul(pV[:], avg[:], sq[:, cc % 2], start=True, stop=True).then_inc(v_fill, 1)
                    V.up()

                for cc in range(CT):
                    pe.wait_ge(o_in[cc % OSLOTS], n * (CT // OSLOTS * 16) + (cc // OSLOTS + 1) * 16)
                    pe.wait_ge(u_read, U.at() + 1)
                    nc.tensor.matmul(pU[:, cc % 2], cen[:], o_c[:, cc % OSLOTS], start=True, stop=True).then_inc(u_fill, 1)
                    U.up()
                    if cc:
                        variance(cc - 1)
                variance(CT - 1)
                for s in range(SUB):
                    at = slice(s * P, (s + 1) * P)
                    pe.wait_ge(v_read, V.at() + 1)
                    for m in range(ND):
                        last = nc.tensor.matmul(pV[:, 0:HID], hid[:, m, at], w_d[:, m], start=(m == 0), stop=(m == ND - 1))
                    last.then_inc(v_fill, 1)
                    V.up()
                    for e2 in range(EXPERTS // 2):
                        pe.wait_ge(e_read, EE.at() + 1)
                        for e in (2 * e2, 2 * e2 + 1):
                            last = nc.tensor.matmul(pE[:, (e2 + 1) % 2, (e % 2) * HID:(e % 2 + 1) * HID], hid[:, ND + e, at], w_d[:, ND + e], start=True, stop=True)
                        last.then_inc(e_fill, 1)
                        EE.up()
                    if s == 0:
                        pe.wait_ge(og_done, n * CT + CT + 2)
                    pe.wait_ge(s_read, SS.at() + 1)
                    for h in range(H):
                        last = nc.tensor.matmul(pS[:, 0:HID], og[:, h, at], w_o[:, h], start=(h == 0), stop=(h == H - 1))
                    last.then_inc(s_fill, 1)
                    SS.up()

            pe.wait_ge(w_in, NW)
            pe.wait_ge(w_scaled, 5 * KT)
            with pe.Fori(0, TILES // 2) as j:
                for c in counts:
                    c.enter(j)
                tile(j, 0)
                tile(j, 1)
            for c in counts:
                c.leave(TILES // 2)

        @block.scalar
        def _(act):
            def tile(n):
                act.wait_ge(exp_in, n + 1)
                nc.scalar.activation(lg[:, 1], lg[:, 0], ACT.Exp).then_inc(exp_done, 1)
                for m in range(HIDDEN):
                    act.wait_ge(a_fill, n * (HIDDEN + H) + m + 1)
                    act.wait_ge(u_read, n * (HIDDEN + CT) + m + 1)
                    nc.scalar.activation(hg[:, m % 2], pA[:, m % 2], ACT.Gelu_apprx_tanh).then_inc(a_read, 1)
                for h in range(H):
                    act.wait_ge(a_fill, n * (HIDDEN + H) + HIDDEN + h + 1)
                    nc.scalar.activation(gate[:, h], pA[:, h % 2], ACT.Sigmoid).then_inc(a_read, 1)

                def deviation(cc):
                    act.wait_ge(v_fill, n * (CT + SUB) + cc + 1)
                    nc.scalar.activation(sd[:, cc % 2], pV[:], ACT.Sqrt, bias=eps[:]).then_inc(v_read, 1)

                for cc in range(CT):
                    act.wait_ge(u_fill, n * (HIDDEN + CT) + HIDDEN + cc + 1)
                    nc.scalar.activation(sq[:, cc % 2], pU[:, cc % 2], ACT.Square).then_inc(sq_done, 1)
                    if cc:
                        deviation(cc - 1)
                deviation(CT - 1)
                for s in range(SUB):
                    act.wait_ge(v_fill, n * (CT + SUB) + CT + s + 1)
                    nc.scalar.activation(dn[:, s], pV[:, 0:HID], ACT.Copy).then_inc(v_read, 1)
                for s in range(SUB):
                    nc_wait = n * SUB + s + 1
                    act.wait_ge(mo_done, nc_wait)
                    for k, src in ((0, dn), (1, mo)):
                        if k == 0:
                            act.wait_ge(v_read, n * (CT + SUB) + CT + s + 2)
                        last = nc.scalar.activation(junk2[:, k], src[:, s], ACT.Square, accum_out=ss[:, k, s:s + 1])
                        last.then_inc(act_chain, 1)
                        act.wait_ge(act_chain, (n * SUB + s) * 2 + k + 1)
                act.wait_ge(ms_ready, n * 2 + 1)
                nc.scalar.activation(rr[:, 0:2], rr[:, 0:2], ACT.Sqrt).then_inc(rms_done, 1)
                for s in range(SUB):
                    act.wait_ge(y_ready, n * SUB + s + 1)
                    nc.scalar.activation(junk2[:, 0], mo[:, s], ACT.Square, accum_out=ss[:, 2, s:s + 1]).then_inc(ssy_done, 1)
                    act.wait_ge(ssy_done, n * SUB + s + 1)
                act.wait_ge(ms_ready, n * 2 + 2)
                nc.scalar.activation(rr[:, 2], rr[:, 2], ACT.Sqrt).then_inc(rms_done, 1)
                act.wait_ge(y_done, n * 2 + 1)
                nc.scalar.activation(mo[:], dn[:], ACT.Silu).then_inc(y_done, 1)

            act.wait_ge(eps_set, 1)
            act.sem_inc(a_read, 2)
            act.sem_inc(v_read, 1)
            with act.Fori(0, TILES) as n:
                tile(n)

        @block.vector
        def _(dve):
            link = Link(dve, chain)
            TT, TS, STT = nc.vector.tensor_tensor, nc.vector.tensor_scalar, nc.vector.scalar_tensor_tensor

            def then(ins):
                link.hold(link.put(ins))

            def router(n):
                l, p, c, one1, p2, one2 = (lg[:, k] for k in range(6))
                def wide(v):
                    return v.unsqueeze(2).to_broadcast([P, SUB, EXPERTS])
                rk = rank[:].unsqueeze(1).to_broadcast([P, SUB, EXPERTS])
                dve.wait_ge(e_fill, n * (1 + SUB * EXPERTS // 2) + 1)
                src = pE[:, 0, 0:SUB * EXPERTS].rearrange("p (s e) -> p s e", s=SUB)
                then(nc.vector.tensor_reduce(rs[:, 0], src, AX.X, ALU.max))
                TT(l, src, wide(rs[:, 0]), ALU.subtract).then_inc(e_read, 1)
                dve.wait_ge(e_read, n * (1 + SUB * EXPERTS // 2) + 3)
                dve.sem_inc(exp_in, 1)
                dve.wait_ge(exp_done, n + 1)
                then(nc.vector.tensor_reduce(rs[:, 1], p, AX.X, ALU.add))
                then(nc.vector.reciprocal(rs[:, 1], rs[:, 1]))
                then(TT(p, p, wide(rs[:, 1]), ALU.mult))
                then(nc.vector.tensor_reduce(rs[:, 2], p, AX.X, ALU.max))
                then(TT(c, p, wide(rs[:, 2]), ALU.is_equal))
                then(TT(c, c, rk, ALU.mult))
                then(nc.vector.tensor_reduce(rs[:, 3], c, AX.X, ALU.max))
                then(TT(one1, c, wide(rs[:, 3]), ALU.is_equal))
                then(STT(p2, one1, -2.0, p, ALU.mult, ALU.add))
                then(nc.vector.tensor_reduce(rs[:, 4], p2, AX.X, ALU.max))
                then(TT(c, p2, wide(rs[:, 4]), ALU.is_equal))
                then(TT(c, c, rk, ALU.mult))
                then(nc.vector.tensor_reduce(rs[:, 5], c, AX.X, ALU.max))
                then(TT(one2, c, wide(rs[:, 5]), ALU.is_equal))
                then(TT(one1, one1, one2, ALU.add))
                then(TT(p, p, one1, ALU.mult))
                then(TT(rs[:, 6], rs[:, 2], rs[:, 4], ALU.add))
                then(nc.vector.reciprocal(rs[:, 6], rs[:, 6]))
                then(TT(p, p, wide(rs[:, 6]), ALU.mult))
                then(TT(aff[:], p, pes[:].unsqueeze(1).to_broadcast([P, SUB, EXPERTS]), ALU.mult))

            def tile(n):
                router(n)
                for m in range(HIDDEN):
                    dve.wait_ge(a_read, n * (HIDDEN + H) + m + 3)
                    dve.wait_ge(u_fill, n * (HIDDEN + CT) + m + 1)
                    TT(hid[:, m], hg[:, m % 2], pU[:, m % 2], ALU.mult).then_inc(u_read, 1)
                for cc in range(CT):
                    dve.wait_ge(v_read, n * (CT + SUB) + cc + 2)
                    then(nc.vector.reciprocal(sd[:, cc % 2], sd[:, cc % 2]))
                    dve.wait_ge(og_done, n * CT + cc + 1)
                    TT(cn[:, cc % 2], pU[:, cc % 2], sd[:, cc % 2], ALU.mult).then_inc(u_read, 1)
                    dve.wait_ge(u_read, n * (HIDDEN + CT) + HIDDEN + cc + 3)
                    TS(cn[:, cc % 2], cn[:, cc % 2], ln[:, 0:1], ln[:, 1:2], ALU.mult, ALU.add).then_inc(cn_ready, 1)
                for s in range(SUB):
                    for e2 in range(EXPERTS // 2):
                        dve.wait_ge(e_fill, n * (1 + SUB * EXPERTS // 2) + 1 + s * EXPERTS // 2 + e2 + 1)
                        for e in (2 * e2, 2 * e2 + 1):
                            src = pE[:, (e2 + 1) % 2, (e % 2) * HID:(e % 2 + 1) * HID]
                            if e == 0:
                                ins = TS(mo[:, s], src, aff[:, s, e:e + 1], None, ALU.mult)
                            else:
                                ins = STT(mo[:, s], src, aff[:, s, e:e + 1], mo[:, s], ALU.mult, ALU.add)
                            if e % 2 == 0:
                                then(ins)
                            elif e < EXPERTS - 1:
                                ins.then_inc(e_read, 1)
                                dve.wait_ge(e_read, n * (1 + SUB * EXPERTS // 2) + 1 + s * EXPERTS // 2 + e2 + 3)
                            else:
                                ins.then_inc(e_read, 1)
                                dve.wait_ge(e_read, n * (1 + SUB * EXPERTS // 2) + 1 + s * EXPERTS // 2 + e2 + 3)
                                dve.sem_inc(mo_done, 1)
                    dve.wait_ge(s_fill, n * SUB + s + 1)
                    dve.wait_ge(out_stored, n * 16 + 16)
                    nc.vector.tensor_copy(s_t[:, s], pS[:, 0:HID]).then_inc(s_read, 1)
                dve.wait_ge(act_chain, (n + 1) * SUB * 2)
                TS(rr[:, 0:2], ss[:, 0:2], 1.0 / HID, 1e-6, ALU.mult, ALU.add).then_inc(ms_ready, 1)
                dve.wait_ge(rms_done, n * 2 + 1)
                then(nc.vector.reciprocal(rr[:, 0:2], rr[:, 0:2]))
                for s in range(SUB):
                    link.put(STT(dn[:, s], dn[:, s], rr[:, 0, s:s + 1], post[:, 0], ALU.mult, ALU.mult))
                    then(STT(mo[:, s], mo[:, s], rr[:, 1, s:s + 1], post[:, 1], ALU.mult, ALU.mult))
                    TT(mo[:, s], mo[:, s], dn[:, s], ALU.add).then_inc(y_ready, 1)
                dve.wait_ge(ssy_done, n * SUB + SUB)
                TS(rr[:, 2], ss[:, 2], 1.0 / HID, 1e-6, ALU.mult, ALU.add).then_inc(ms_ready, 1)
                dve.wait_ge(rms_done, n * 2 + 2)
                then(nc.vector.reciprocal(rr[:, 2], rr[:, 2]))
                for s in range(SUB):
                    ins = STT(dn[:, s], mo[:, s], rr[:, 2, s:s + 1], post[:, 2], ALU.mult, ALU.mult)
                ins.then_inc(y_done, 1)
                dve.wait_ge(y_done, n * 2 + 2)
                dve.wait_ge(s_read, n * SUB + SUB + 1)
                then(TT(s_t[:], s_t[:], mo[:], ALU.mult))
                dve.wait_ge(x_in, n * 16 + 16)
                TT(s_t[:], s_t[:], x_t[:], ALU.add).then_inc(out_ready, 1)
                link.restart()

            dve.sem_inc(u_read, 2)
            dve.sem_inc(e_read, 2)
            dve.sem_inc(s_read, 1)
            dve.wait_ge(w_in, NW)
            for k in range(KT):
                TS(w_g[:, k, 0:ND], w_g[:, k, 0:ND], pre[:, k, 0:1], None, ALU.mult).then_inc(w_scaled, 1)
                TS(w_u[:, k, 0:ND], w_u[:, k, 0:ND], pre[:, k, 0:1], None, ALU.mult).then_inc(w_scaled, 1)
                TS(w_g[:, k, ND:], w_g[:, k, ND:], pre[:, k, 1:2], None, ALU.mult).then_inc(w_scaled, 1)
                TS(w_u[:, k, ND:], w_u[:, k, ND:], pre[:, k, 1:2], None, ALU.mult).then_inc(w_scaled, 1)
                TS(w_r[:, k], w_r[:, k], pre[:, k, 2:3], float(HID) ** -0.5, ALU.mult, ALU.mult).then_inc(w_scaled, 1)
            with dve.Fori(0, TILES) as n:
                tile(n)


SCRATCH = {
    "xnT": (P, KT, TOK), "xrT": (P, KT, TOK), "beta": (H, TOK),
    "kq": (BATCH, NCH + 1, P, H, 2 * C), "va": (BATCH, NCH, P, H, 2 * C), "o": (BATCH, NCH, P, H, C),
}


def declare(nc, arrays, shown=()):
    io = {n: nc.dram_tensor("in_" + n, v.shape, mybir.dt.from_np(v.dtype), kind="ExternalInput").ap() for n, v in arrays.items()}
    io["out"] = nc.dram_tensor("out", (TOK, HID), fp32, kind="ExternalOutput").ap()
    scratch = {n: nc.dram_tensor("scr_" + n, s, fp32, kind="ExternalOutput" if n in shown else "Internal").ap() for n, s in SCRATCH.items()}
    return io, scratch


def layouts(i):
    import numpy as np

    def heads(w):
        return np.ascontiguousarray(w.reshape(H, D, -1).transpose(1, 0, 2))

    a = {}
    g = lambda n: np.asarray(i["L0_attn_" + n])
    f = lambda n: np.asarray(i["L0_ffn_" + n])
    a["x"] = g("x").reshape(TOK, HID)
    wall = np.stack([g("Wq"), g("Wk"), g("Wv"), g("Wa")])
    wall = wall.reshape(4, H, D, KT, P).transpose(1, 4, 3, 0, 2).reshape(H, P, KT * 4 * P)
    a["Wqkva"] = np.ascontiguousarray(np.concatenate([wall, wall[-1:]]))
    a["WbT"] = np.ascontiguousarray(g("Wb").T)
    a["bb"] = g("bb").reshape(H, 1)
    a["par"] = np.concatenate([heads(g("qc_w")), heads(g("kc_w")), heads(g("vc_w")), heads(g("qc_b")), heads(g("kc_b")), heads(g("vc_b")), heads(g("ba"))], axis=2)
    a["ident"] = np.eye(P, dtype=np.float32)
    row = np.arange(P)
    a["sel"] = np.ascontiguousarray(np.broadcast_to((row[:, None] % BL == np.arange(BL))[:, :, None], (P, BL, P))).astype(np.float32)
    a["mask"] = np.ascontiguousarray(np.broadcast_to((row[:, None] // BL == np.arange(H))[:, :, None], (P, H, 2 * BL))).astype(np.float32)
    a["rank"] = np.ascontiguousarray(np.broadcast_to(np.arange(EXPERTS, 0, -1), (P, EXPERTS))).astype(np.float32)
    a["cen"] = (np.eye(P) - 1.0 / P).astype(np.float32)
    a["avg"] = np.full((P, P), 1.0 / P, np.float32)
    a["ln"] = np.stack([g("ln_g"), g("ln_b")], axis=1)
    a["WgT"] = np.ascontiguousarray(g("Wg").T)
    a["WoT"] = np.ascontiguousarray(g("Wo").T)
    a["pre"] = np.stack([f("rn_pre1"), f("rn_pre2"), f("router_scale")], axis=1)
    a["post"] = np.concatenate([f("rn_post1"), f("rn_post2"), f("rn_post")])
    a["pes"] = f("per_expert_scale")
    for n in ("w_gate", "w_up", "w_down", "router_w", "we_gate", "we_up", "we_down"):
        a[n] = f(n)
    return a


def kernel(**inputs):
    import concourse.bacc as _bacc
    from concourse.bass_utils import run_bass_kernel_spmd as _run

    nc = _bacc.Bacc("TRN2", target_bir_lowering=False, num_devices=1)
    arrays = layouts(inputs)
    build(nc, *declare(nc, arrays))
    r = _run(nc, [{"in_" + n: v for n, v in arrays.items()}], core_ids=[0])
    return r.results[0]["out"].reshape(BATCH, SEQ, HID)
```

```python
import concourse.bass as bass
from concourse import mybir
from contextlib import ExitStack

BATCH, SEQ, HID = 2, 2048, 256
TOK = BATCH * SEQ
H, D = 16, 128
P = 128
KT = HID // P
TAPS = 4
C = 32
NCH = SEQ // C
BL = 8
NBL = C // BL
LEAD = C - BL
NT = 512
INNER = 1024
EXPERTS, MI = 8, 128
QD = 4
NG = H // QD

fp32 = mybir.dt.float32
ALU = mybir.AluOpType
ACT = mybir.ActivationFunctionType
AX = mybir.AxisListType


def build(nc, io, scratch):
    with ExitStack() as top:
        with ExitStack() as st:
            xnT = st.enter_context(nc.sbuf_tensor("xnT", [P, KT, TOK], fp32))
            normalise_and_transpose(nc, io, scratch, xnT)
            project_and_convolve(nc, io, scratch, xnT)
        recurrence(nc, io, scratch)
        ffn_and_output(nc, io, scratch)


def normalise_and_transpose(nc, io, scratch, xnT):
    NTILE = TOK // P
    with ExitStack() as st:
        def sb(name, shape):
            return st.enter_context(nc.sbuf_tensor(name, shape, fp32))

        def sem(name):
            return st.enter_context(nc.semaphore(name))

        x_sb = sb("x_sb", [P, NTILE, HID])
        xrT = sb("xrT", [P, KT, TOK])
        ident = sb("identA", [P, P])
        wb = sb("wb", [P, KT, H])
        bb = sb("bb", [H, 1])
        stats = sb("stats", [P, NTILE, 6])
        mv = sb("mv", [P, NTILE, 2])
        rstd = sb("rstd", [P, NTILE])
        shift = sb("shift", [P, NTILE])
        sumsq = sb("sumsq", [P, NTILE])
        rrms = sb("rrms", [P, NTILE])
        squares = sb("squares", [P, HID])
        tiles = sb("tiles", [P, 2, 2, HID])
        beta = sb("beta", [H, TOK])
        pT = st.enter_context(nc.psum_tensor("pT", [P, 2, 2, NT], fp32))
        pB = st.enter_context(nc.psum_tensor("pB", [P, 2, NT], fp32))

        x_in, const_in = sem("x_in"), sem("constA_in")
        stats_step, stats_done = sem("stats_step"), sem("stats_done")
        rstd_done = sem("rstd_done")
        sumsq_done, rrms_done = sem("sumsq_done"), sem("rrms_done")
        xn_ready, xr_ready = sem("xn_ready"), sem("xr_ready")
        tile_free, turned = sem("tile_free"), sem("turned")
        xnT_copied, xrT_copied = sem("xnT_copied"), sem("xrT_copied")
        turn_free = sem("turn_free")
        beta_mm, beta_done, stored = sem("beta_mm"), sem("beta_done"), sem("storedA")
        block = st.enter_context(nc.Block())

        @block.sync
        def _(sp):
            sp.dma_start(x_sb[:], io["x"].rearrange("(n p) c -> p n c", p=P)).then_inc(x_in, 16)
            sp.dma_start(ident[:], io["ident"]).then_inc(const_in, 16)
            sp.dma_start(wb[:], io["WbT"].rearrange("(k p) h -> p k h", p=P)).then_inc(const_in, 16)
            sp.dma_start(bb[:], io["bb"]).then_inc(const_in, 16)
            sp.wait_ge(xnT_copied, NTILE + 1)
            sp.dma_start(scratch["xnT"], xnT[:]).then_inc(stored, 16)
            sp.wait_ge(xrT_copied, NTILE + 1)
            sp.dma_start(scratch["xrT"], xrT[:]).then_inc(stored, 16)
            sp.wait_ge(beta_done, TOK // NT + 1)
            sp.dma_start(scratch["beta"], beta[:]).then_inc(stored, 16)
            sp.wait_ge(stored, 48)

        @block.vector
        def _(dve):
            dve.wait_ge(x_in, 16)
            with dve.Fori(0, NTILE) as n:
                nc.vector.bn_stats(stats[:, bass.ds(n, 1), :], x_sb[:, bass.ds(n, 1), :]).then_inc(stats_step, 1)
            dve.wait_ge(stats_step, NTILE)
            for n in range(NTILE):
                nc.vector.bn_aggr(mv[:, n, :], stats[:, n, :]).then_inc(stats_step, 1)
            dve.wait_ge(stats_step, 2 * NTILE)
            nc.vector.tensor_scalar(rstd[:].unsqueeze(2), mv[:, :, 1:2], 1e-5, None, ALU.add).then_inc(stats_step, 1)
            dve.wait_ge(rstd_done, 1)
            nc.vector.reciprocal(rstd[:], rstd[:]).then_inc(rstd_done, 1)
            dve.wait_ge(rstd_done, 2)
            nc.vector.scalar_tensor_tensor(shift[:], mv[:, :, 0], -1.0, rstd[:], ALU.mult, ALU.mult).then_inc(stats_done, 1)
            dve.wait_ge(sumsq_done, NTILE)
            nc.vector.tensor_scalar(rrms[:], sumsq[:], 1.0 / HID, 1e-6, ALU.mult, ALU.add).then_inc(rrms_done, 1)
            dve.wait_ge(rrms_done, 2)
            nc.vector.reciprocal(rrms[:], rrms[:]).then_inc(rrms_done, 1)
            dve.wait_ge(rrms_done, 3)
            dve.wait_ge(stats_done, 1)

            def copy_xr(n, slot):
                dve.wait_ge(turned, n + 1)
                nc.vector.tensor_copy(xrT[:, :, bass.ds(n * P, P)], pT[:, slot, 1, 0:KT * P].rearrange("p (k t) -> p k t", k=KT)).then_inc(xrT_copied, 1)

            with dve.Fori(0, NTILE // 2) as j:
                for slot in range(2):
                    n = j * 2 + slot
                    dve.wait_ge(tile_free, n + 1)
                    nc.vector.tensor_scalar(tiles[:, slot, 0, :].unsqueeze(1), x_sb[:, bass.ds(n, 1), :], rstd[:, bass.ds(n, 1)], shift[:, bass.ds(n, 1)], ALU.mult, ALU.add).then_inc(xn_ready, 1)
                    dve.wait_ge(xn_ready, n + 1)
                    nc.vector.tensor_scalar(tiles[:, slot, 1, :], tiles[:, slot, 0, :], rrms[:, bass.ds(n, 1)], None, ALU.mult).then_inc(xr_ready, 1)
                    copy_xr(n, slot)

        @block.scalar
        def _(act):
            act.wait_ge(stats_step, 2 * NTILE + 1)
            nc.scalar.activation(rstd[:], rstd[:], ACT.Sqrt).then_inc(rstd_done, 1)
            act.wait_ge(stats_done, 1)
            with act.Fori(0, NTILE) as n:
                nc.scalar.activation(squares[:].unsqueeze(1), x_sb[:, bass.ds(n, 1), :], ACT.Square, bias=shift[:, bass.ds(n, 1)], scale=rstd[:, bass.ds(n, 1)],
                                     accum_out=sumsq[:, bass.ds(n, 1)]).then_inc(sumsq_done, 1)
                act.wait_ge(sumsq_done, n + 1)
                act.wait_ge(stats_done, 1)
            act.wait_ge(rrms_done, 1)
            nc.scalar.activation(rrms[:], rrms[:], ACT.Sqrt).then_inc(rrms_done, 1)
            with act.Fori(0, NTILE // 2) as j:
                for slot in range(2):
                    n = j * 2 + slot
                    act.wait_ge(turned, n + 1)
                    nc.scalar.activation(xnT[:, :, bass.ds(n * P, P)], pT[:, slot, 0, 0:KT * P].rearrange("p (k t) -> p k t", k=KT), ACT.Copy).then_inc(xnT_copied, 1)
            act.wait_ge(const_in, 48)
            with act.Fori(0, TOK // NT // 2) as j:
                for slot in range(2):
                    act.wait_ge(beta_mm, j * 2 + slot + 1)
                    nc.scalar.activation(beta[:, bass.ds((j * 2 + slot) * NT, NT)], pB[0:H, slot, :], ACT.Sigmoid, bias=bb[:]).then_inc(beta_done, 1)

        @block.tensor
        def _(pe):
            pe.sem_inc(tile_free, 2)
            for free in (xnT_copied, xrT_copied, beta_done):
                pe.sem_inc(free, 1)
            pe.wait_ge(const_in, 48)
            with pe.Fori(0, NTILE // 2) as j:
                for slot in range(2):
                    n = j * 2 + slot
                    pe.wait_ge(xr_ready, n + 1)
                    if slot == 0:
                        pe.wait_ge(xnT_copied, j * 2 + 1)
                        pe.wait_ge(xrT_copied, j * 2 + 1)
                    for half in range(2):
                        for k in range(KT):
                            last = nc.tensor.transpose(pT[:, slot, half, k * P:(k + 1) * P], tiles[:, slot, half, k * P:(k + 1) * P], ident[:])
                    last.then_inc(turned, 1)
                    pe.wait_ge(turned, n + 1)
                    pe.sem_inc(tile_free, 1)
            pe.wait_ge(xnT_copied, NTILE + 1)
            with pe.Fori(0, TOK // NT // 2) as j:
                for slot in range(2):
                    if slot == 0:
                        pe.wait_ge(beta_done, j * 2 + 1)
                    for k in range(KT):
                        last = nc.tensor.matmul(pB[0:H, slot, :], wb[:, k, :], xnT[:, k, bass.ds((j * 2 + slot) * NT, NT)], start=(k == 0), stop=(k == KT - 1))
                    last.then_inc(beta_mm, 1)


def project_and_convolve(nc, io, scratch, xnT):
    QV, KV, VV, AV = range(4)
    ORDER = (KV, QV, VV, AV)
    NCONV = 3 * BATCH
    NUNIT = 4 * BATCH
    NN = SEQ // NT
    with ExitStack() as st:
        def sb(name, shape):
            return st.enter_context(nc.sbuf_tensor(name, shape, fp32))

        def sem(name):
            return st.enter_context(nc.semaphore(name))

        w_stage = sb("w_stage", [P, KT * 4 * P])
        w = sb("w", [P, KT, 4, P])
        par = sb("par", [P, H, 16])
        ba = sb("ba", [P, 1])
        raw = sb("raw", [P, 2, TAPS - 1 + SEQ])
        acc = sb("acc", [P, 2, SEQ])
        kq = sb("kqA", [P, BATCH, (NCH + 1) * C, 2])
        va = sb("vaA", [P, BATCH, NCH, 2, C])
        ps = st.enter_context(nc.psum_tensor("psA", [P, 2, NN, NT], fp32))

        par_in, w_in, w_ready, w_used = sem("par_in"), sem("w_in"), sem("w_ready"), sem("w_used")
        mm, ps_free = sem("mmA"), sem("psA_free")
        pad, raw_ready, raw_free = sem("pad"), sem("raw_ready"), sem("raw_free")
        conv_step, conv_ready, acc_free = sem("conv_step"), sem("conv_ready"), sem("acc_free")
        ba_ready = sem("ba_ready")
        gate_done = sem("gate_done")
        kq_stored, va_stored = sem("kq_stored"), sem("va_stored")
        block = st.enter_context(nc.Block())

        @block.sync
        def _(sp):
            for stored in (kq_stored, va_stored):
                sp.sem_inc(stored, 16)
            sp.dma_start(par[:], io["par"]).then_inc(par_in, 16)
            sp.dma_start(w_stage[:], io["Wqkva"][0]).then_inc(w_in, 16)
            with sp.Fori(0, H) as h:
                sp.wait_ge(w_ready, h + 1)
                nxt = sp.snap(h + 1)
                silus = [sp.snap(h * NCONV + r + 2) for r in range(NCONV)]
                sp.dma_start(w_stage[:], io["Wqkva"][bass.ds(nxt, 1)].rearrange("o p n -> p (o n)")).then_inc(w_in, 16)
                for b in range(BATCH):
                    sp.wait_ge(acc_free, silus[3 * b + 1])
                    sp.dma_start(scratch["kq"][b, :, :, bass.ds(h, 1), :].rearrange("c p h n -> p c (h n)"),
                                 kq[:, b].rearrange("p (c t) e -> p c (t e)", t=C)).then_inc(kq_stored, 16)
                    sp.wait_ge(acc_free, silus[3 * b + 2])
                    sp.dma_start(scratch["va"][b, :, :, bass.ds(h, 1), :].rearrange("c p h n -> p c (h n)"),
                                 va[:, b].rearrange("p c e t -> p c (e t)")).then_inc(va_stored, 16)
            sp.wait_ge(kq_stored, 16 * H * BATCH + 16)
            sp.wait_ge(va_stored, 16 * H * BATCH + 16)
            sp.wait_ge(w_in, 16 * (H + 1))

        @block.gpsimd
        def _(pool):
            nc.gpsimd.memset(raw[:, :, 0:TAPS - 1], 0.0).then_inc(pad, 1)
            nc.gpsimd.memset(kq[:, :, 0:LEAD], 0.0).then_inc(pad, 1)
            nc.gpsimd.memset(kq[:, :, LEAD + SEQ:], 0.0).then_inc(pad, 1)

        @block.tensor
        def _(pe):
            with pe.Fori(0, H) as h:
                pe.wait_ge(w_ready, h + 1)
                for b in range(BATCH):
                    for j, u in enumerate(ORDER):
                        unit = 4 * b + j
                        pe.wait_ge(ps_free, h * NUNIT + unit + 1)
                        for n in range(NN):
                            for k in range(KT):
                                t0 = b * SEQ + n * NT
                                last = nc.tensor.matmul(ps[:, unit % 2, n, :], w[:, k, u, :], xnT[:, k, t0:t0 + NT], start=(k == 0), stop=(k == KT - 1))
                            last.then_inc(mm, 1)
                pe.wait_ge(mm, (h + 1) * NUNIT * NN)
                pe.sem_inc(w_used, 1)

        @block.scalar
        def _(act):
            act.sem_inc(ps_free, 2)
            act.sem_inc(acc_free, 1)
            act.wait_ge(par_in, 16)

            def silu(h, b, v):
                row = 3 * b + v
                act.wait_ge(conv_ready, h * NCONV + row + 1)
                src = acc[:, row % 2, :]
                if v == 0:
                    act.wait_ge(kq_stored, h * 32 + 16)
                if v == 2:
                    act.wait_ge(va_stored, h * 32 + 16)
                if v < 2:
                    dst = kq[:, b, LEAD:LEAD + SEQ, v]
                else:
                    dst, src = va[:, b, :, 0, :], src.rearrange("p (c t) -> p c t", t=C)
                nc.scalar.activation(dst, src, ACT.Silu).then_inc(acc_free, 1)

            with act.Fori(0, H) as h:
                nc.scalar.activation(ba[:], par[:, bass.ds(h, 1), 15], ACT.Copy).then_inc(ba_ready, 1)
                act.wait_ge(ba_ready, h + 1)
                for b in range(BATCH):
                    for j, u in enumerate(ORDER):
                        unit = 4 * b + j
                        if u != AV:
                            row = 3 * b + j
                            act.wait_ge(raw_free, h * NCONV + row + 1)
                            for n in range(NN):
                                act.wait_ge(mm, h * NUNIT * NN + unit * NN + n + 1)
                                nc.scalar.activation(raw[:, row % 2, TAPS - 1 + n * NT:TAPS - 1 + (n + 1) * NT], ps[:, unit % 2, n, :], ACT.Copy).then_inc(raw_ready, 1)
                            act.wait_ge(raw_ready, (h * NCONV + row + 1) * NN)
                            act.sem_inc(ps_free, 1)
                        else:
                            act.wait_ge(va_stored, h * 32 + 16)
                            for n in range(NN):
                                act.wait_ge(mm, h * NUNIT * NN + unit * NN + n + 1)
                                last = nc.scalar.activation(va[:, b, n * NT // C:(n + 1) * NT // C, 1, :], ps[:, unit % 2, n, :].rearrange("p (c t) -> p c t", t=C),
                                                            ACT.Sigmoid, bias=ba[:])
                            last.then_inc(gate_done, 1)
                            act.wait_ge(gate_done, h * BATCH + b + 1)
                            act.sem_inc(ps_free, 1)
                        if j:
                            silu(h, b, j - 1)

        @block.vector
        def _(dve):
            dve.sem_inc(raw_free, 2)
            dve.wait_ge(par_in, 16)
            dve.wait_ge(pad, 3)
            dve.wait_ge(w_in, 16)
            nc.vector.tensor_copy(w[:].rearrange("p k u n -> p (k u n)"), w_stage[:]).then_inc(w_ready, 1)
            with dve.Fori(0, H) as h:
                for b in range(BATCH):
                    for v, u in enumerate(ORDER[:3]):
                        row = 3 * b + v
                        dve.wait_ge(raw_ready, (h * NCONV + row + 1) * NN)
                        if row >= 2:
                            dve.wait_ge(acc_free, h * NCONV + row)
                        else:
                            dve.wait_ge(acc_free, h * NCONV + 1)
                        out = acc[:, row % 2, :]
                        tap = lambda k: par[:, bass.ds(h, 1), TAPS * u + k]
                        nc.vector.tensor_scalar(out, raw[:, row % 2, 0:SEQ], tap(0), par[:, bass.ds(h, 1), 12 + u], ALU.mult, ALU.add).then_inc(conv_step, 1)
                        for k in range(1, TAPS):
                            dve.wait_ge(conv_step, h * (NCONV * 3) + row * 3 + k)
                            ins = nc.vector.scalar_tensor_tensor(out, raw[:, row % 2, k:k + SEQ], tap(k), out, ALU.mult, ALU.add)
                            ins.then_inc(conv_step if k < TAPS - 1 else conv_ready, 1)
                        dve.wait_ge(conv_ready, h * NCONV + row + 1)
                        dve.sem_inc(raw_free, 1)
                        if row == NCONV - 2:
                            dve.wait_ge(w_used, h + 1)
                            dve.wait_ge(w_in, h * 16 + 32)
                            nc.vector.tensor_copy(w[:].rearrange("p k u n -> p (k u n)"), w_stage[:]).then_inc(w_ready, 1)


def act_fills(last=False):
    order = []
    for B in range(NBL):
        for b in range(BATCH):
            order.append(("turn", b, B))
            if (B, b) == (0, 0):
                order += [("add", 0, g) for g in range(NG)]
            if (B, b) in ((0, 1), (1, 0)):
                order += [("state", 1 - b, g) for g in range(NG)]
                order += [("base", 1 - b, 0), ("base", 1 - b, 1)]
            if (B, b) == (0, 1):
                order += [("add", 1, g) for g in range(NG)]
            if B >= 2 and not last:
                order.append(("kg" if b else "kT", B - 2, 0))
    return order


class Count:

    def __init__(self, turn):
        self.turn, self.start, self.n, self.i = turn, 0, 0, None

    def enter(self, i):
        self.start, self.n, self.i = self.start + self.n, 0, i

    def leave(self, turns):
        assert self.n == self.turn, (self.n, self.turn)
        self.start, self.n, self.i = self.start + turns * self.turn, 0, None

    def at(self, back=0):
        v = self.start + self.n - back
        return v if self.i is None else self.i * self.turn + v

    def up(self):
        self.n += 1
        return self.at()


class Link:

    def __init__(self, dve, sem):
        self.dve, self.sem, self.n = dve, sem, 0

    def put(self, ins):
        ins.then_inc(self.sem, 1)
        self.n += 1
        return self.n

    def hold(self, n):
        self.dve.wait_ge(self.sem, n)

    def restart(self):
        self.hold(self.n)
        self.dve.sem_clear(self.sem)
        self.n = 0


def recurrence(nc, io, scratch):
    PAIRS = NCH // 2
    FILLS = act_fills()
    PRE_ORDER = [(what, b, 0) for b in range(BATCH) for what in ("kT", "kg")]
    PRE_FILLS = len(PRE_ORDER)
    OWNS_BEFORE = BATCH * (NBL - 1)
    ZEROED = 9
    BETA = 1.0 / D
    OSCALE = float(D) ** 0.5
    width = [2 * BL - 1 - 2 * t for t in range(BL)]
    bank_of = [0, 0, 1, 1, 1, 1, 0, 0]
    col_of, used = [], [0, 0]
    for t in range(BL):
        col_of.append(used[bank_of[t]])
        used[bank_of[t]] += H * width[t]
    assert max(used) <= NT

    with ExitStack() as st:
        def sb(name, shape):
            return st.enter_context(nc.sbuf_tensor(name, shape, fp32))

        def pb(name, shape):
            return st.enter_context(nc.psum_tensor(name, shape, fp32))

        def sem(name):
            return st.enter_context(nc.semaphore(name))

        def sems(name):
            return [sem(f"{name}{b}") for b in range(BATCH)]

        kq = sb("kq", [P, 2, BATCH, H, C, 2])
        va = sb("va", [P, 2, BATCH, H, 2, C])
        own = sb("own", [P, 2, BATCH, NBL, H, 2 * BL])
        kr = sb("kr", [P, BATCH, H, C])
        kown = sb("kown", [P, BATCH, NBL, H, BL])
        kg = sb("kg", [P, 2, BATCH, NG, QD, 2 * C])
        kT = sb("kT", [P, 2, BATCH, NG, QD, D])
        S = sb("S", [P, BATCH, H, D])
        ST = sb("ST", [P, BATCH, H, D])
        base = sb("base", [P, BATCH, H, 2 * C])
        U = sb("U", [P, BATCH, NG, NT])
        X = sb("X", [P, BATCH, 2, H, 2 * BL])
        Y = sb("Y", [P, BATCH, H * (2 * BL - 1)])
        E = sb("E", [P, BATCH, H, C])
        ET = sb("ET", [P, BATCH, NG, D])
        dsuf = sb("dsuf", [P, 2, BATCH, H, NBL, BL])
        dblk = sb("dblk", [P, 2, BATCH, H, NBL])
        dcum = sb("dcum", [P, 2, BATCH, H, NBL])
        o = sb("o", [P, 2, BATCH, H, C])
        sel = sb("sel", [P, BL, P])
        ident = sb("identB", [P, P])
        mask = sb("mask", [P, H, 2 * BL])
        bown = sb("bown", [P, BATCH, SEQ // BL])
        b32 = sb("b32", [P, BATCH, NG, NCH])
        bt_own = sb("bt_own", [P, BATCH, 2, H, BL])
        bt_32 = sb("bt_32", [NCH, BATCH, H, C])
        unit = sb("unit", [P, 2])
        b32c = sb("b32c", [P, BATCH, NG])
        psel = pb("psel", [P, BATCH, 2, NT])
        pact = pb("pact", [P, 2, NT])
        phist = pb("phist", [P, NT])
        pown = pb("pown", [P, NT])

        consts_in, beta_in, zeroed = sem("consts_in"), sem("beta_in"), sem("zeroed")
        beta_turned, beta_scaled = sem("beta_turned"), sem("beta_scaled")
        kq_in, va_in = [sems("kq_in_s0_"), sems("kq_in_s1_")], [sems("va_in_s0_"), sems("va_in_s1_")]
        act_fill, act_evac = sem("act_fill"), sem("act_evac")
        own_fill, own_evac = sem("own_fill"), sem("own_evac")
        hist_fill, hist_evac = sem("hist_fill"), sem("hist_evac")
        sel_ready, sel_used = sems("sel_ready"), sems("sel_used")
        e_ready, x_done = sems("e_ready"), sems("x_done")
        decay_step, decay_ready, s_added = sem("decay_step"), sems("decay_ready"), sems("s_added")
        o_copied, o_stored, chain = sems("o_copied"), [sems("o_stored_s0_"), sems("o_stored_s1_")], sem("chain")
        b32c_ready, k_laid, x_begun, past_done = sem("b32c_ready"), sems("k_laid"), sems("x_begun"), sems("past_done")
        block = st.enter_context(nc.Block())

        def evacs(c, tag, b, n, last=False):
            return c * len(FILLS) + PRE_FILLS + act_fills(last).index((tag, b, n)) + 1

        @block.sync
        def _(sp):
            def load(c, slot, b):
                sp.dma_start(kq[:, slot, b].rearrange("p h t e -> p (h t e)"), scratch["kq"][b, bass.ds(c + 1, 1)].rearrange("c p h n -> p (c h n)")).then_inc(kq_in[slot][b], 16)

            def load_va(c, slot, b):
                sp.dma_start(va[:, slot, b].rearrange("p h e t -> p (h e t)"), scratch["va"][b, bass.ds(c, 1)].rearrange("c p h n -> p (c h n)")).then_inc(va_in[slot][b], 16)

            sp.dma_start(ident[:], io["ident"]).then_inc(consts_in, 16)
            sp.dma_start(sel[:], io["sel"]).then_inc(consts_in, 16)
            sp.dma_start(mask[:], io["mask"]).then_inc(consts_in, 16)
            for b in range(BATCH):
                load(-1, 1, b)
                load(0, 0, b)
                load_va(0, 0, b)
            for b in range(BATCH):
                row = scratch["beta"][:, b * SEQ:(b + 1) * SEQ]
                for half in range(2):
                    part = row[:, half * P * BL:(half + 1) * P * BL]
                    sp.dma_start(bt_own[:, b, half], part.rearrange("h (n s) -> n h s", s=BL)).then_inc(beta_in, 16)
                sp.dma_start(bt_32[:, b], row.rearrange("h (c s) -> c h s", s=C)).then_inc(beta_in, 16)
            for b in range(BATCH):
                load_va(1, 1, b)
            sp.wait_ge(own_fill, BATCH)
            for b in range(BATCH):
                load(1, 1, b)

            def store(c, slot, b):
                sp.dma_start(scratch["o"][b, bass.ds(c, 1)].rearrange("c p h n -> p (c h n)"), o[:, slot, b].rearrange("p h t -> p (h t)")).then_inc(o_stored[slot][b], 16)

            def chunk(c, slot, more):
                for b in range(BATCH):
                    if more:
                        sp.wait_ge(own_fill, OWNS_BEFORE + c * BATCH * NBL + BATCH + b + 1)
                        load(c + 2, slot, b)
                for b in range(BATCH):
                    if more:
                        sp.wait_ge(x_done[b], c * NBL + NBL)
                        load_va(c + 2, slot, b)
                    sp.wait_ge(o_copied[b], c * NBL + NBL + 2)
                    store(c, slot, b)

            for b in range(BATCH):
                for slot in range(2):
                    sp.sem_inc(o_stored[slot][b], 16)
            with sp.Fori(0, PAIRS - 1) as i:
                chunk(i * 2, 0, True)
                chunk(i * 2 + 1, 1, True)
            chunk(NCH - 2, 0, False)
            chunk(NCH - 1, 1, False)
            for b in range(BATCH):
                for slot in range(2):
                    sp.wait_ge(o_stored[slot][b], PAIRS * 16 + 16)

        @block.gpsimd
        def _(pool):
            PER = BL + NBL

            for t in (S, E, kT, kg, base, dcum):
                nc.gpsimd.memset(t[:], 0.0).then_inc(zeroed, 1)
            nc.gpsimd.memset(dsuf[:].rearrange("p s b h n t -> p (s b h n) t")[:, :, BL - 1], 1.0).then_inc(zeroed, 1)
            nc.gpsimd.memset(unit[:, 0:1], 1.0).then_inc(zeroed, 1)
            nc.gpsimd.memset(unit[:, 1:2], OSCALE).then_inc(zeroed, 1)
            pool.wait_ge(zeroed, ZEROED)
            for b in range(BATCH):
                pool.sem_inc(o_copied[b], 2)
                pool.sem_inc(past_done[b], 1)

            def decays(c, slot, b, loads):
                k = (c * BATCH + b) * (PER - 1)
                pool.wait_ge(va_in[slot][b], loads * 16)
                a = va[:, slot, b, :, 1, :].rearrange("p h (n s) -> p h n s", s=BL)
                f = dsuf[:, slot, b]
                chained = [(f[:, :, :, s], f[:, :, :, s + 1], a[:, :, :, s + 1]) for s in range(BL - 2, -1, -1)]
                chained += [(dblk[:, slot, b], f[:, :, :, 0], a[:, :, :, 0]), (dcum[:, slot, b, :, 0], dblk[:, slot, b, :, 0], f[:, :, 0, BL - 1])]
                chained += [(dcum[:, slot, b, :, n], dcum[:, slot, b, :, n - 1], dblk[:, slot, b, :, n]) for n in range(1, NBL)]
                for n, (out, x, y) in enumerate(chained):
                    if n:
                        pool.wait_ge(decay_step, k + n)
                    nc.gpsimd.tensor_tensor(out, x, y, ALU.mult).then_inc(decay_step if n < PER - 1 else decay_ready[b], 1)
                assert len(chained) == PER

            def lay_keys(slot, b, loads):
                pool.wait_ge(kq_in[slot][b], loads * 16)
                one = unit[:, 0:1].unsqueeze(2)
                nc.gpsimd.tensor_tensor(kr[:, b, :, 0:BL], kq[:, 1 - slot, b, :, LEAD:C, 0], one.to_broadcast([P, H, BL]), ALU.mult)
                nc.gpsimd.tensor_tensor(kr[:, b, :, BL:C], kq[:, slot, b, :, 0:LEAD, 0], one.to_broadcast([P, H, LEAD]), ALU.mult)
                for B in range(NBL):
                    src = kq[:, slot, b, :, (B - 1) * BL:B * BL, 0] if B else kq[:, 1 - slot, b, :, LEAD:C, 0]
                    last = nc.gpsimd.tensor_tensor(kown[:, b, B], src, one.to_broadcast([P, H, BL]), ALU.mult)
                last.then_inc(k_laid[b], 1)

            def begin(c, slot, b, B):
                if B == 1:
                    pool.wait_ge(decay_ready[b], c + 1)
                    pool.wait_ge(act_evac, evacs(c, "base", b, 1))
                slot, n = (slot, B - 1) if B else (1 - slot, NBL - 1)
                nc.gpsimd.tensor_tensor(X[:, b, B % 2], base[:, b, :, n * 2 * BL:(n + 1) * 2 * BL], dcum[:, slot, b, :, n:n + 1].to_broadcast([P, H, 2 * BL]), ALU.mult).then_inc(x_begun[b], 1)

            def decay_past(c, slot, b, B, last):
                pool.wait_ge(act_fill, evacs(c, "turn", b, B, last))
                past = E[:, b, :, 0:B * BL]
                nc.gpsimd.tensor_tensor(past, past, dblk[:, slot, b, :, B:B + 1].to_broadcast([P, H, B * BL]), ALU.mult).then_inc(past_done[b], 1)

            def add_state(c, b):
                for g in range(NG):
                    pool.wait_ge(act_evac, evacs(c, "add", b, g))
                    part = S[:, b, g * QD:(g + 1) * QD].rearrange("p q n -> p (q n)")
                    nc.gpsimd.tensor_tensor(part, part, U[:, b, g], ALU.add).then_inc(s_added[b], 1)

            def chunk(c, slot, last, turn):
                for B in range(NBL):
                    if B == 0:
                        add_state(c, 0)
                        if not last:
                            pool.wait_ge(own_fill, OWNS_BEFORE + c * BATCH * NBL + BATCH)
                            for b in range(BATCH):
                                lay_keys(1 - slot, b, turn + 2)
                        add_state(c, 1)
                    for b in range(BATCH):
                        if B == 0:
                            pool.wait_ge(o_stored[slot][b], turn * 16 + 16)
                        else:
                            decay_past(c, slot, b, B, last)
                        if B == 1 and not last:
                            pool.wait_ge(decay_ready[b], c + 1)
                            pool.wait_ge(act_evac, evacs(c, "state", b, NG - 1))
                            nc.gpsimd.tensor_tensor(S[:, b], S[:, b], dcum[:, slot, b, :, NBL - 1:NBL].to_broadcast([P, H, D]), ALU.mult)
                        if B == 2 and not last:
                            decays(c + 1, 1 - slot, b, turn + slot + 1)
                        pool.wait_ge(x_done[b], c * NBL + B + 1)
                        nc.gpsimd.tensor_tensor(o[:, slot, b, :, B * BL:(B + 1) * BL], X[:, b, B % 2].rearrange("p h (t e) -> p h t e", e=2)[:, :, :, 1],
                                                unit[:, 1:2].unsqueeze(2).to_broadcast([P, H, BL]), ALU.mult).then_inc(o_copied[b], 1)
                        if B < NBL - 1:
                            begin(c, slot, b, B + 1)
                        elif not last:
                            begin(c + 1, 1 - slot, b, 0)

            for b in range(BATCH):
                pool.wait_ge(kq_in[1][b], 16)
                lay_keys(0, b, 1)
                decays(0, 0, b, 1)
                begin(0, 0, b, 0)
            with pool.Fori(0, PAIRS - 1) as i:
                chunk(i * 2, 0, False, i)
                chunk(i * 2 + 1, 1, False, i)
            chunk(NCH - 2, 0, False, PAIRS - 1)
            chunk(NCH - 1, 1, True, PAIRS - 1)

        @block.scalar
        def _(act):
            def betas(c):
                nc.scalar.activation(b32c[:].unsqueeze(3), b32[:, :, :, bass.ds(c, 1)], ACT.Copy).then_inc(b32c_ready, 1)
                act.wait_ge(b32c_ready, c + 1)

            def evac(c, tag, b, n, bank, slot):
                src = pact[:, bank]
                if tag == "base":
                    if n == 0:
                        act.wait_ge(x_begun[b], c * NBL + 1)
                    last = nc.scalar.activation(base[:, b, n * H // 2:(n + 1) * H // 2].rearrange("p h n -> p (h n)"), src, ACT.Copy)
                elif tag == "add":
                    last = nc.scalar.activation(U[:, b, n], src, ACT.Copy)
                elif tag == "turn":
                    last = nc.scalar.activation(ET[:, b].rearrange("p g n -> p (g n)"), src, ACT.Copy)
                elif tag == "state":
                    last = nc.scalar.activation(ST[:, b, n * QD:(n + 1) * QD].rearrange("p q n -> p (q n)"), src, ACT.Copy)
                elif tag == "kT":
                    for g in range(NG):
                        for Q in range(QD):
                            rows = slice(Q * C, (Q + 1) * C)
                            last = nc.scalar.activation(kT[rows, slot, b, g, Q], src[rows, g * D:(g + 1) * D], ACT.Copy, scale=b32c[rows, b, g:g + 1])
                else:
                    for g in range(NG):
                        for Q in range(QD):
                            rows = slice(Q * C, (Q + 1) * C)
                            last = nc.scalar.activation(kg[rows, slot, b, g, Q], src[rows, g * 2 * C:(g + 1) * 2 * C], ACT.Copy, scale=b32c[rows, b, g:g + 1])
                last.then_inc(act_evac, 1)

            def chunk(c, slot, last):
                for n, (tag, b, k) in enumerate(act_fills(last)):
                    act.wait_ge(act_fill, c * len(FILLS) + PRE_FILLS + n + 1)
                    if (tag, b) == ("kT", 0):
                        betas(c + 1)
                    evac(c, tag, b, k, (PRE_FILLS + n) % 2, 1 - slot)

            act.wait_ge(beta_turned, 1)
            nc.scalar.activation(bown[:].rearrange("p b n -> p (b n)"), pact[:, 0], ACT.Copy, scale=BETA).then_inc(beta_scaled, 1)
            nc.scalar.activation(b32[:].rearrange("p b g c -> p (b g c)"), pact[:, 1], ACT.Copy, scale=BETA).then_inc(beta_scaled, 1)
            act.wait_ge(beta_scaled, 2)
            act.wait_ge(zeroed, ZEROED)
            betas(0)
            for n, (tag, b, k) in enumerate(PRE_ORDER):
                act.wait_ge(act_fill, n + 1)
                evac(0, tag, b, k, n % 2, 0)
            with act.Fori(0, PAIRS - 1) as i:
                chunk(i * 2, 0, False)
                chunk(i * 2 + 1, 1, False)
            chunk(NCH - 2, 0, False)
            chunk(NCH - 1, 1, True)

        @block.tensor
        def _(pe):
            owns, hists = Count(2 * BATCH * NBL), Count(2 * BATCH * NBL)
            fills = Count(2 * len(FILLS))

            def act_bank():
                bank = (fills.start + fills.n) % 2
                if fills.i is not None or fills.start + fills.n >= 2:
                    pe.wait_ge(act_evac, fills.at(1))
                return pact[:, bank]

            def filled(last):
                last.then_inc(act_fill, 1)
                fills.up()

            def turn_E(b):
                dst = act_bank()
                for g in range(NG):
                    last = nc.tensor.transpose(dst[:, g * P:(g + 1) * P], E[:, b, g * QD:(g + 1) * QD].rearrange("p h s -> p (h s)"), ident[:])
                filled(last)
                return fills.at()

            def bases(slot, b):
                for half in range(2):
                    dst = act_bank()
                    for h in range(H // 2):
                        hh = half * H // 2 + h
                        last = nc.tensor.matmul(dst[:, h * 2 * C:(h + 1) * 2 * C], ST[:, b, hh], kq[:, slot, b, hh].rearrange("p t e -> p (t e)"), start=True, stop=True)
                    filled(last)

            def keys_T(b):
                dst = act_bank()
                for g in range(NG):
                    last = nc.tensor.transpose(dst[:, g * P:(g + 1) * P], kr[:, b, g * QD:(g + 1) * QD].rearrange("p h t -> p (h t)"), ident[:])
                filled(last)

            def keys_by_pairs(slot, b):
                dst = act_bank()
                for g in range(NG):
                    for Q in range(QD):
                        h = g * QD + Q
                        last = nc.tensor.matmul(dst[Q * C:(Q + 1) * C, g * 2 * C:(g + 1) * 2 * C], kr[:, b, h], kq[:, slot, b, h].rearrange("p t e -> p (t e)"),
                                                start=True, stop=True, tile_position=(0, Q * C))
                filled(last)

            def own_bank():
                if owns.i is not None or owns.start + owns.n:
                    pe.wait_ge(own_evac, owns.at())
                return pown

            def own_block(slot, b, B):
                dst = own_bank()
                pairs = kq[:, slot, b, :, (B - 1) * BL:B * BL] if B else kq[:, 1 - slot, b, :, LEAD:C]
                nc.tensor.matmul(dst[:, 0:H * 2 * BL], kown[:, b, B].rearrange("p h s -> p (h s)"), pairs.rearrange("p h t e -> p h (t e)"),
                                 start=True, stop=True).then_inc(own_fill, 1)
                owns.up()

            def sel_bank(c, slot, b, B, bank):
                pe.wait_ge(sel_used[b], (c * NBL + B) * 2 + 2)
                for t in range(BL):
                    if bank_of[t] == bank:
                        last = nc.tensor.matmul(psel[:, b, bank, col_of[t]:col_of[t] + H * width[t]], sel[:, t], own[:, slot, b, B, :, 2 * t + 1:2 * BL], start=True, stop=True)
                last.then_inc(sel_ready[b], 1)

            def history(slot, b, B, turned):
                pe.wait_ge(act_evac, turned)
                pe.wait_ge(hist_evac, hists.at() + 1)
                slot, n = (slot, B - 1) if B else (1 - slot, NBL - 1)
                for g in range(NG):
                    last = nc.tensor.matmul(phist[:, g * QD * 2 * BL:(g + 1) * QD * 2 * BL], ET[:, b, g], kg[:, slot, b, g, :, n * 2 * BL:(n + 1) * 2 * BL], start=True, stop=True)
                last.then_inc(hist_fill, 1)
                hists.up()

            def adds(slot, b):
                for g in range(NG):
                    dst = act_bank()
                    filled(nc.tensor.matmul(dst, ET[:, b, g], kT[:, 1 - slot, b, g].rearrange("p q n -> p (q n)"), start=True, stop=True))

            def state_T(c, b, groups):
                for g in groups:
                    pe.wait_ge(s_added[b], c * NG + g + 1)
                    dst = act_bank()
                    for Q in range(QD):
                        last = nc.tensor.transpose(dst[:, Q * P:(Q + 1) * P], S[:, b, g * QD + Q], ident[:])
                    filled(last)

            def chunk(c, slot, last, next_loads):
                for B in range(NBL):
                    for b in range(BATCH):
                        pe.wait_ge(e_ready[b], c * NBL + B + 1)
                        if B != 1:
                            pe.wait_ge(past_done[b], c * (NBL - 1) + (B if B else 1))
                        turned = turn_E(b)
                        sel_bank(c, slot, b, B, 0)
                        history(slot, b, B, turned)
                        if B >= 2 and not last:
                            if b == 0:
                                keys_T(B - 2)
                            else:
                                keys_by_pairs(1 - slot, B - 2)
                        update = (B, b) in ((0, 1), (1, 0))
                        if update:
                            state_T(c, 1 - b, range(0, 2))
                        sel_bank(c, slot, b, B, 1)
                        if update:
                            state_T(c, 1 - b, range(2, NG))
                        if (B, b) == (0, 0):
                            adds(slot, 0)
                        if B == 0:
                            own_block(slot, b, NBL - 1)
                        elif not last:
                            if B == 1:
                                pe.wait_ge(kq_in[1 - slot][b], next_loads * 16)
                                pe.wait_ge(k_laid[b], c + 2)
                            own_block(1 - slot, b, B - 1)
                        if update:
                            bases(slot, 1 - b)
                        if (B, b) == (0, 1):
                            adds(slot, 1)
            pe.wait_ge(consts_in, 48)
            pe.wait_ge(beta_in, 16 * 3 * BATCH)
            for b in range(BATCH):
                for half in range(2):
                    at = (b * 2 + half) * P
                    nc.tensor.transpose(pact[:, 0, at:at + P], bt_own[:, b, half].rearrange("n h s -> n (h s)"), ident[:])
                for g in range(NG):
                    at = (b * NG + g) * NCH
                    last = nc.tensor.transpose(pact[:, 1, at:at + NCH], bt_32[:, b, g * QD:(g + 1) * QD].rearrange("c h s -> c (h s)"), ident[0:NCH, 0:NCH])
            last.then_inc(beta_turned, 1)
            pe.wait_ge(beta_scaled, 2)
            pe.wait_ge(zeroed, ZEROED)
            for b in range(BATCH):
                pe.wait_ge(kq_in[0][b], 16)
                pe.wait_ge(kq_in[1][b], 16)
                pe.wait_ge(k_laid[b], 1)
                keys_T(b)
                keys_by_pairs(0, b)
            for B in range(NBL - 1):
                for b in range(BATCH):
                    own_block(0, b, B)
            pe.wait_ge(own_evac, OWNS_BEFORE)
            assert fills.n == PRE_FILLS
            with pe.Fori(0, PAIRS - 1) as i:
                for k in (owns, hists, fills):
                    k.enter(i)
                chunk(i * 2, 0, False, i + 2)
                chunk(i * 2 + 1, 1, False, i + 2)
            for k in (owns, hists, fills):
                k.leave(PAIRS - 1)
            chunk(NCH - 2, 0, False, PAIRS + 1)
            chunk(NCH - 1, 1, True, 0)

        @block.vector
        def _(dve):
            owns, hists = Count(2 * BATCH * NBL), Count(2 * BATCH * NBL)
            link = Link(dve, chain)

            def own_out(col, slot, b, B):
                dve.wait_ge(own_fill, owns.up())
                nc.vector.scalar_tensor_tensor(own[:, slot, b, B], pown[:, 0:H * 2 * BL].rearrange("p (h n) -> p h n", h=H), bown[:, b, bass.ds(col, 1)] if not isinstance(col, int) else bown[:, b, col:col + 1],
                                               mask[:], ALU.mult, ALU.mult).then_inc(own_evac, 1)

            def block_steps(c, slot, b, B, between):
                Xb, v, a = X[:, b, B % 2], va[:, slot, b, :, 0], va[:, slot, b, :, 1]
                filled = hists.up()
                dve.wait_ge(hist_fill, filled)
                dve.wait_ge(e_ready[b], c * NBL + B + 1)
                dve.wait_ge(x_begun[b], c * NBL + B + 1)
                nc.vector.tensor_tensor(Xb, Xb, phist[:, 0:H * 2 * BL].rearrange("p (h n) -> p h n", h=H), ALU.add).then_inc(hist_evac, 1)
                if B == 0:
                    link.hold(link.put(nc.vector.memset(E[:, b, :, BL:], 0.0)))
                dve.wait_ge(hist_evac, filled + 1)
                for t in range(BL):
                    if t in (0, 2):
                        dve.wait_ge(sel_ready[b], (c * NBL + B) * 2 + (1 if t == 0 else 2))
                    s, w = B * BL + t, width[t]
                    if t:
                        link.hold(x_now)
                    e = E[:, b, :, s:s + 1]
                    e_now = link.put(nc.vector.tensor_tensor(e, v[:, :, s:s + 1], Xb[:, :, 2 * t:2 * t + 1], ALU.subtract))
                    rest = Xb[:, :, 2 * t + 1:2 * BL]
                    xa_now = link.put(nc.vector.tensor_tensor(rest, rest, a[:, :, s:s + 1].to_broadcast([P, H, w]), ALU.mult))
                    y = Y[:, b, 0:H * w].rearrange("p (h n) -> p h n", h=H)
                    kgt = psel[:, b, bank_of[t], col_of[t]:col_of[t] + H * w].rearrange("p (h n) -> p h n", h=H)
                    link.hold(e_now)
                    ins = nc.vector.tensor_tensor(y, kgt, e.to_broadcast([P, H, w]), ALU.mult)
                    if t in (5, 7):
                        ins.then_inc(sel_used[b], 1)
                        if t in between:
                            between[t]()
                        dve.wait_ge(sel_used[b], (c * NBL + B) * 2 + (3 if t == 5 else 4))
                        link.hold(xa_now)
                    else:
                        y_now = link.put(ins)
                        if t in between:
                            between[t]()
                        link.hold(y_now)
                    ins = nc.vector.tensor_tensor(rest, rest, y, ALU.add)
                    if t < BL - 1:
                        x_now = link.put(ins)
                    else:
                        ins.then_inc(x_done[b], 1)
                mine = E[:, b, :, B * BL:(B + 1) * BL]
                nc.vector.tensor_tensor(mine, mine, dsuf[:, slot, b, :, B], ALU.mult).then_inc(e_ready[b], 1)

            def chunk(c, slot, last, loads):
                for B in range(NBL):
                    for b in range(BATCH):
                        if B == 0:
                            dve.wait_ge(va_in[slot][b], loads * 16)
                            dve.wait_ge(decay_ready[b], c + 1)

                        def own_next():
                            own_out(c * NBL + NBL - 1 + B, 1 - slot if B else slot, b, (B - 1) % NBL)

                        block_steps(c, slot, b, B, {3: own_next} if B == 0 or not last else {})
                link.restart()

            for b in range(BATCH):
                dve.sem_inc(sel_used[b], 2)
                dve.sem_inc(e_ready[b], 1)
            dve.sem_inc(hist_evac, 1)
            dve.wait_ge(consts_in, 48)
            dve.wait_ge(beta_scaled, 2)
            dve.wait_ge(zeroed, ZEROED)
            for B in range(NBL - 1):
                for b in range(BATCH):
                    own_out(B, 0, b, B)
            with dve.Fori(0, PAIRS - 1) as i:
                for k in (owns, hists):
                    k.enter(i)
                chunk(i * 2, 0, False, i + 1)
                chunk(i * 2 + 1, 1, False, i + 1)
            for k in (owns, hists):
                k.leave(PAIRS - 1)
            chunk(NCH - 2, 0, False, PAIRS)
            chunk(NCH - 1, 1, True, PAIRS)


def ffn_and_output(nc, io, scratch):
    TILES = TOK // NT
    SUB = NT // P
    CT = NT // C
    HIDDEN = INNER // P + EXPERTS
    ND = INNER // P
    OSLOTS = 4
    with ExitStack() as st:
        def sb(name, shape):
            return st.enter_context(nc.sbuf_tensor(name, shape, fp32))

        def pb(name, shape):
            return st.enter_context(nc.psum_tensor(name, shape, fp32))

        def sem(name):
            return st.enter_context(nc.semaphore(name))

        w_g = sb("w_g", [P, KT, HIDDEN, P])
        w_u = sb("w_u", [P, KT, HIDDEN, P])
        w_d = sb("w_d", [P, HIDDEN, HID])
        w_r = sb("w_r", [P, KT, EXPERTS])
        wg_a = sb("wg_a", [P, KT, H * D])
        w_o = sb("w_o", [P, H, HID])
        pre = sb("pre", [P, KT, 3])
        post = sb("post", [P, 3, HID])
        pes = sb("pes", [P, EXPERTS])
        rank = sb("rank", [P, EXPERTS])
        ln = sb("ln", [P, 2])
        eps = sb("eps", [P, 1])
        cen = sb("cen", [P, P])
        avg = sb("avg", [P, 1])
        ident = sb("identC", [P, P])
        xr = sb("xr", [P, 2, KT, NT])
        xn = sb("xn", [P, 2, KT, NT])
        hg = sb("hg", [P, 2, NT])
        hid = sb("hid", [P, HIDDEN, NT])
        gate = sb("gate", [P, H, NT])
        o_c = sb("o_c", [P, OSLOTS, NT])
        sq = sb("sq", [P, 2, NT])
        sd = sb("sd", [P, CT * SUB])
        rsd = sb("rsd", [P, CT * SUB])
        ctr = hid
        assert CT == HIDDEN == H
        cn = sb("cn", [P, 2, NT])
        og = gate
        lg = sb("lg", [P, 6, SUB, EXPERTS])
        rs = sb("rs", [P, 8, SUB])
        aff = sb("aff", [P, SUB, EXPERTS])
        x_t = sb("x_t", [P, SUB, HID])
        dn = sb("dn", [P, SUB, HID])
        mo = sb("mo", [P, SUB, HID])
        s_t = sb("s_t", [P, SUB, HID])
        junk2 = sb("junk2", [P, 2, HID])
        ss = sb("ss", [P, 3, SUB])
        rr = sb("rr", [P, 3, SUB])
        pA = pb("pA", [P, 2, NT])
        pU = pb("pU", [P, 2, NT])
        pV = pb("pV", [P, NT])
        pS = pb("pS", [P, NT])
        pE = pb("pE", [P, 2, NT])

        w_in, w_scaled, eps_set = sem("wC_in"), sem("w_scaled"), sem("eps_set")
        xt_in, x_in = [sem("xt_in0"), sem("xt_in1")], sem("xC_in")
        o_in = [sem(f"o_in{k}") for k in range(OSLOTS)]
        a_fill, a_read = sem("a_fill"), sem("a_read")
        u_fill, u_read = sem("u_fill"), sem("u_read")
        v_fill, v_read = sem("v_fill"), sem("v_read")
        s_fill, s_read = sem("s_fill"), sem("s_read")
        e_fill, e_read = sem("e_fill"), sem("e_read")
        sq_done, og_done = sem("sq_done"), sem("og_done")
        c_read, rsd_ready, r_fill, r_read = sem("c_read"), sem("rsd_ready"), sem("r_fill"), sem("r_read")
        exp_in, exp_done = sem("exp_in"), sem("exp_done")
        mo_done, ms_ready, rms_done = sem("mo_done"), sem("ms_ready"), sem("rms_done")
        ssy_done, y_ready, y_done = sem("ssy_done"), sem("y_ready"), sem("y_done")
        out_ready, out_stored, chain, act_chain = sem("out_ready"), sem("out_stored"), sem("chainC"), sem("act_chain")
        block = st.enter_context(nc.Block())
        NW = 16 * 19

        @block.sync
        def _(sp):
            wide = lambda name: io[name].rearrange("(k p) n -> p k n", p=P)
            sp.dma_start(w_g[:, :, 0:ND].rearrange("p k n m -> p k (n m)"), wide("w_gate")).then_inc(w_in, 16)
            sp.dma_start(w_u[:, :, 0:ND].rearrange("p k n m -> p k (n m)"), wide("w_up")).then_inc(w_in, 16)
            for k in range(KT):
                sp.dma_start(w_g[:, k, ND:], io["we_gate"][:, k * P:(k + 1) * P, :].rearrange("e p m -> p e m")).then_inc(w_in, 16)
                sp.dma_start(w_u[:, k, ND:], io["we_up"][:, k * P:(k + 1) * P, :].rearrange("e p m -> p e m")).then_inc(w_in, 16)
            sp.dma_start(w_d[:, 0:ND], io["w_down"].rearrange("(n p) c -> p n c", p=P)).then_inc(w_in, 16)
            sp.dma_start(w_d[:, ND:], io["we_down"].rearrange("e p c -> p e c")).then_inc(w_in, 16)
            sp.dma_start(w_r[:], wide("router_w")).then_inc(w_in, 16)
            sp.dma_start(wg_a[:], wide("WgT")).then_inc(w_in, 16)
            sp.dma_start(w_o[:], io["WoT"].rearrange("(h p) c -> p h c", p=P)).then_inc(w_in, 16)
            sp.dma_start(pre[:], io["pre"].rearrange("(k p) n -> p k n", p=P)).then_inc(w_in, 16)
            sp.dma_start(post[:].rearrange("p n c -> p (n c)"), io["post"].partition_broadcast(P)).then_inc(w_in, 16)
            sp.dma_start(pes[:], io["pes"].partition_broadcast(P)).then_inc(w_in, 16)
            for t, name in ((rank, "rank"), (ln, "ln"), (cen, "cen"), (avg, "avg"), (ident, "ident")):
                sp.dma_start(t[:], io[name]).then_inc(w_in, 16)

            def tile(j, slot, n):
                at = n * NT
                sp.dma_start(xr[:, slot], scratch["xrT"][:, :, bass.ds(at, NT)]).then_inc(xt_in[slot], 16)
                sp.dma_start(xn[:, slot], scratch["xnT"][:, :, bass.ds(at, NT)]).then_inc(xt_in[slot], 16)

            def chunk_load(n, cc, free):
                if free is not None:
                    sp.wait_ge(u_fill, free)
                sp.dma_start(o_c[:, cc % OSLOTS], scratch["o"][:].rearrange("b c p h t -> (b c) p (h t)")[bass.ds(n * CT + cc, 1)].rearrange("c p n -> p (c n)")).then_inc(o_in[cc % OSLOTS], 16)

            def store(n):
                sp.wait_ge(out_ready, n + 1)
                sp.dma_start(io["out"].rearrange("(n s p) c -> n p s c", p=P, s=SUB)[bass.ds(n, 1)].rearrange("n p s c -> p (n s) c"), s_t[:]).then_inc(out_stored, 16)

            def load_tile(j, slot, n, before):
                tile(j, slot, n)
                for cc in range(CT):
                    if cc >= OSLOTS:
                        chunk_load(n, cc, n * (HIDDEN + CT) + cc - OSLOTS + 1)
                    else:
                        chunk_load(n, cc, None if before is None else n * (HIDDEN + CT) - HIDDEN)
                if before is not None:
                    store(before)
                sp.dma_start(x_t[:], io["x"].rearrange("(n s p) c -> n p s c", p=P, s=SUB)[bass.ds(n, 1)].rearrange("n p s c -> p (n s) c")).then_inc(x_in, 16)

            sp.sem_inc(out_stored, 16)
            load_tile(0, 0, 0, None)
            with sp.Fori(0, TILES // 2 - 1) as j:
                load_tile(j, 1, j * 2 + 1, j * 2)
                load_tile(j + 1, 0, j * 2 + 2, j * 2 + 1)
            load_tile(TILES // 2 - 1, 1, TILES - 1, TILES - 2)
            store(TILES - 1)
            sp.wait_ge(out_stored, TILES * 16 + 16)

        @block.gpsimd
        def _(pool):
            nc.gpsimd.memset(eps[:], 1e-5).then_inc(eps_set, 1)

        @block.tensor
        def _(pe):
            A, U, V, SS, EE = Count(2 * (HIDDEN + H)), Count(2 * (HIDDEN + CT)), Count(2 * (1 + SUB)), Count(2 * SUB), Count(2 * (1 + SUB * EXPERTS // 2))
            counts = (A, U, V, SS, EE)

            def tile(j, slot):
                n = j * 2 + slot
                pe.wait_ge(xt_in[slot], j * 32 + 32)
                pe.wait_ge(e_read, EE.at() + 2)
                for s in range(SUB):
                    for k in range(KT):
                        last = nc.tensor.matmul(pE[:, 0, s * EXPERTS:(s + 1) * EXPERTS], xr[:, slot, k, s * P:(s + 1) * P], w_r[:, k], start=(k == 0), stop=(k == KT - 1))
                last.then_inc(e_fill, 1)
                EE.up()

                def variance(cc):
                    pe.wait_ge(sq_done, n * CT + cc + 1)
                    if cc == 0:
                        pe.wait_ge(v_read, V.at() + 1)
                    for g in range(SUB):
                        last = nc.tensor.matmul(pV[:, cc * SUB + g:cc * SUB + g + 1], sq[:, cc % 2, g * P:(g + 1) * P], avg[:], start=True, stop=True)
                    if cc == CT - 1:
                        last.then_inc(v_fill, 1)
                        V.up()

                pe.wait_ge(u_read, n * HIDDEN + 2)
                for h in range(H):
                    pe.wait_ge(a_read, A.at() + 1)
                    for k in range(KT):
                        last = nc.tensor.matmul(pA[:, h % 2], wg_a[:, k, h * D:(h + 1) * D], xn[:, slot, k], start=(k == 0), stop=(k == KT - 1))
                    last.then_inc(a_fill, 1)
                    A.up()
                    pe.wait_ge(o_in[h % OSLOTS], n * (CT // OSLOTS * 16) + (h // OSLOTS + 1) * 16)
                    pe.wait_ge(c_read, n * CT + h + 1)
                    nc.tensor.matmul(pU[:, h % 2], cen[:], o_c[:, h % OSLOTS], start=True, stop=True).then_inc(u_fill, 1)
                    U.up()
                    if h:
                        variance(h - 1)
                variance(CT - 1)
                pe.wait_ge(c_read, n * CT + CT + 2)
                for m in range(HIDDEN):
                    pe.wait_ge(a_read, A.at() + 1)
                    for k in range(KT):
                        last = nc.tensor.matmul(pA[:, m % 2], w_g[:, k, m], xr[:, slot, k], start=(k == 0), stop=(k == KT - 1))
                    last.then_inc(a_fill, 1)
                    A.up()
                    pe.wait_ge(u_read, n * HIDDEN + m + 1)
                    for k in range(KT):
                        last = nc.tensor.matmul(pU[:, m % 2], w_u[:, k, m], xr[:, slot, k], start=(k == 0), stop=(k == KT - 1))
                    last.then_inc(u_fill, 1)
                    U.up()
                    if m == 0:
                        pe.wait_ge(e_read, EE.at() + 2)
                        pe.wait_ge(rsd_ready, n + 1)
                    pe.wait_ge(r_read, n * CT + m + 1)
                    for g in range(SUB):
                        last = nc.tensor.matmul(pE[:, m % 2, g * P:(g + 1) * P], rsd[:, m * SUB + g:m * SUB + g + 1].to_broadcast([P, P]), ident[:], start=True, stop=True)
                    last.then_inc(r_fill, 1)
                pe.wait_ge(r_read, n * CT + CT + 2)
                for s in range(SUB):
                    at = slice(s * P, (s + 1) * P)
                    pe.wait_ge(v_read, V.at() + 1)
                    for m in range(ND):
                        last = nc.tensor.matmul(pV[:, 0:HID], hid[:, m, at], w_d[:, m], start=(m == 0), stop=(m == ND - 1))
                    last.then_inc(v_fill, 1)
                    V.up()
                    for e2 in range(EXPERTS // 2):
                        pe.wait_ge(e_read, EE.at() + 1)
                        for e in (2 * e2, 2 * e2 + 1):
                            last = nc.tensor.matmul(pE[:, (e2 + 1) % 2, (e % 2) * HID:(e % 2 + 1) * HID], hid[:, ND + e, at], w_d[:, ND + e], start=True, stop=True)
                        last.then_inc(e_fill, 1)
                        EE.up()
                    if s == 0:
                        pe.wait_ge(og_done, n * CT + CT)
                    pe.wait_ge(s_read, SS.at() + 1)
                    for h in range(H):
                        last = nc.tensor.matmul(pS[:, 0:HID], og[:, h, at], w_o[:, h], start=(h == 0), stop=(h == H - 1))
                    last.then_inc(s_fill, 1)
                    SS.up()

            pe.wait_ge(w_in, NW)
            pe.wait_ge(w_scaled, 5 * KT)
            with pe.Fori(0, TILES // 2) as j:
                for c in counts:
                    c.enter(j)
                tile(j, 0)
                tile(j, 1)
            for c in counts:
                c.leave(TILES // 2)

        @block.scalar
        def _(act):
            def finish(n):
                act.wait_ge(ms_ready, n * 2 + 1)
                nc.scalar.activation(rr[:, 0:2], rr[:, 0:2], ACT.Sqrt).then_inc(rms_done, 1)
                yield
                for s in range(SUB):
                    act.wait_ge(y_ready, n * SUB + s + 1)
                    nc.scalar.activation(junk2[:, 0], mo[:, s], ACT.Square, accum_out=ss[:, 2, s:s + 1]).then_inc(ssy_done, 1)
                    act.wait_ge(ssy_done, n * SUB + s + 1)
                yield
                act.wait_ge(ms_ready, n * 2 + 2)
                nc.scalar.activation(rr[:, 2], rr[:, 2], ACT.Sqrt).then_inc(rms_done, 1)
                yield
                act.wait_ge(y_done, n * 2 + 1)
                nc.scalar.activation(mo[:], dn[:], ACT.Silu).then_inc(y_done, 1)
                yield

            def tile(n, before):
                act.wait_ge(exp_in, n + 1)
                nc.scalar.activation(lg[:, 1], lg[:, 0], ACT.Exp).then_inc(exp_done, 1)
                tail = finish(n - 1) if before else None
                for h in range(H):
                    if before and h in (2, 5, 8, 11):
                        next(tail)
                    act.wait_ge(a_fill, n * (HIDDEN + H) + h + 1)
                    nc.scalar.activation(gate[:, h], pA[:, h % 2], ACT.Sigmoid).then_inc(a_read, 1)
                    act.wait_ge(u_fill, n * (HIDDEN + CT) + h + 1)
                    nc.scalar.activation(sq[:, h % 2], pU[:, h % 2], ACT.Square).then_inc(sq_done, 1)
                    nc.scalar.activation(ctr[:, h], pU[:, h % 2], ACT.Copy, scale=ln[:, 0:1]).then_inc(c_read, 1)
                act.wait_ge(v_fill, n * (1 + SUB) + 1)
                nc.scalar.activation(sd[:], pV[:, 0:CT * SUB], ACT.Sqrt, bias=eps[:]).then_inc(v_read, 1)
                for m in range(HIDDEN):
                    act.wait_ge(a_fill, n * (HIDDEN + H) + H + m + 1)
                    act.wait_ge(u_read, n * HIDDEN + m + 1)
                    nc.scalar.activation(hg[:, m % 2], pA[:, m % 2], ACT.Gelu_apprx_tanh).then_inc(a_read, 1)
                for s in range(SUB):
                    act.wait_ge(v_fill, n * (1 + SUB) + 1 + s + 1)
                    nc.scalar.activation(dn[:, s], pV[:, 0:HID], ACT.Copy).then_inc(v_read, 1)
                    act.wait_ge(mo_done, n * SUB + s + 1)
                    act.wait_ge(v_read, n * (1 + SUB) + 1 + s + 2)
                    for k, src in ((0, dn), (1, mo)):
                        nc.scalar.activation(junk2[:, k], src[:, s], ACT.Square, accum_out=ss[:, k, s:s + 1]).then_inc(act_chain, 1)
                        act.wait_ge(act_chain, (n * SUB + s) * 2 + k + 1)

            act.wait_ge(eps_set, 1)
            act.sem_inc(c_read, 2)
            act.sem_inc(a_read, 2)
            act.sem_inc(v_read, 1)
            tile(0, False)
            with act.Fori(0, TILES - 1) as i:
                tile(i + 1, True)
            for _ in finish(TILES - 1):
                pass

        @block.vector
        def _(dve):
            link = Link(dve, chain)
            TT, TS, STT = nc.vector.tensor_tensor, nc.vector.tensor_scalar, nc.vector.scalar_tensor_tensor

            def then(ins):
                link.hold(link.put(ins))

            def router(n):
                l, p, c, one1, p2, one2 = (lg[:, k] for k in range(6))
                def wide(v):
                    return v.unsqueeze(2).to_broadcast([P, SUB, EXPERTS])
                rk = rank[:].unsqueeze(1).to_broadcast([P, SUB, EXPERTS])
                dve.wait_ge(e_fill, n * (1 + SUB * EXPERTS // 2) + 1)
                src = pE[:, 0, 0:SUB * EXPERTS].rearrange("p (s e) -> p s e", s=SUB)
                then(nc.vector.tensor_reduce(rs[:, 0], src, AX.X, ALU.max))
                TT(l, src, wide(rs[:, 0]), ALU.subtract).then_inc(e_read, 1)
                dve.wait_ge(e_read, n * (1 + SUB * EXPERTS // 2) + 3)
                dve.sem_inc(exp_in, 1)
                dve.wait_ge(exp_done, n + 1)
                then(nc.vector.tensor_reduce(rs[:, 1], p, AX.X, ALU.add))
                then(nc.vector.reciprocal(rs[:, 1], rs[:, 1]))
                then(TT(p, p, wide(rs[:, 1]), ALU.mult))
                then(nc.vector.tensor_reduce(rs[:, 2], p, AX.X, ALU.max))
                then(TT(c, p, wide(rs[:, 2]), ALU.is_equal))
                then(TT(c, c, rk, ALU.mult))
                then(nc.vector.tensor_reduce(rs[:, 3], c, AX.X, ALU.max))
                then(TT(one1, c, wide(rs[:, 3]), ALU.is_equal))
                then(STT(p2, one1, -2.0, p, ALU.mult, ALU.add))
                then(nc.vector.tensor_reduce(rs[:, 4], p2, AX.X, ALU.max))
                then(TT(c, p2, wide(rs[:, 4]), ALU.is_equal))
                then(TT(c, c, rk, ALU.mult))
                then(nc.vector.tensor_reduce(rs[:, 5], c, AX.X, ALU.max))
                then(TT(one2, c, wide(rs[:, 5]), ALU.is_equal))
                then(TT(one1, one1, one2, ALU.add))
                then(TT(p, p, one1, ALU.mult))
                then(TT(rs[:, 6], rs[:, 2], rs[:, 4], ALU.add))
                then(nc.vector.reciprocal(rs[:, 6], rs[:, 6]))
                then(TT(p, p, wide(rs[:, 6]), ALU.mult))
                then(TT(aff[:], p, pes[:].unsqueeze(1).to_broadcast([P, SUB, EXPERTS]), ALU.mult))

            def finish(n):
                dve.wait_ge(act_chain, (n + 1) * SUB * 2)
                TS(rr[:, 0:2], ss[:, 0:2], 1.0 / HID, 1e-6, ALU.mult, ALU.add).then_inc(ms_ready, 1)
                dve.wait_ge(rms_done, n * 2 + 1)
                then(nc.vector.reciprocal(rr[:, 0:2], rr[:, 0:2]))
                for s in range(SUB):
                    link.put(STT(dn[:, s], dn[:, s], rr[:, 0, s:s + 1], post[:, 0], ALU.mult, ALU.mult))
                    then(STT(mo[:, s], mo[:, s], rr[:, 1, s:s + 1], post[:, 1], ALU.mult, ALU.mult))
                    TT(mo[:, s], mo[:, s], dn[:, s], ALU.add).then_inc(y_ready, 1)
                dve.wait_ge(ssy_done, n * SUB + SUB)
                TS(rr[:, 2], ss[:, 2], 1.0 / HID, 1e-6, ALU.mult, ALU.add).then_inc(ms_ready, 1)
                dve.wait_ge(rms_done, n * 2 + 2)
                then(nc.vector.reciprocal(rr[:, 2], rr[:, 2]))
                for s in range(SUB):
                    ins = STT(dn[:, s], mo[:, s], rr[:, 2, s:s + 1], post[:, 2], ALU.mult, ALU.mult)
                ins.then_inc(y_done, 1)
                dve.wait_ge(y_done, n * 2 + 2)
                dve.wait_ge(s_read, n * SUB + SUB + 1)
                then(TT(s_t[:], s_t[:], mo[:], ALU.mult))
                dve.wait_ge(x_in, n * 16 + 16)
                TT(s_t[:], s_t[:], x_t[:], ALU.add).then_inc(out_ready, 1)

            def tile(n, before):
                router(n)
                if before:
                    finish(n - 1)
                dve.wait_ge(v_read, n * (1 + SUB) + 2)
                nc.vector.reciprocal(rsd[:], sd[:]).then_inc(rsd_ready, 1)
                dve.wait_ge(c_read, n * CT + CT + 2)
                for m in range(HIDDEN):
                    dve.wait_ge(r_fill, n * CT + m + 1)
                    TT(cn[:, m % 2], ctr[:, m], pE[:, m % 2], ALU.mult).then_inc(r_read, 1)
                    dve.wait_ge(r_read, n * CT + m + 3)
                    STT(og[:, :, m * C:(m + 1) * C], cn[:, m % 2].rearrange("p (h t) -> p h t", h=H), ln[:, 1:2], gate[:, :, m * C:(m + 1) * C], ALU.add, ALU.mult).then_inc(og_done, 1)
                    dve.wait_ge(a_read, n * (HIDDEN + H) + H + m + 3)
                    dve.wait_ge(u_fill, n * (HIDDEN + CT) + CT + m + 1)
                    TT(hid[:, m], hg[:, m % 2], pU[:, m % 2], ALU.mult).then_inc(u_read, 1)
                for s in range(SUB):
                    for e2 in range(EXPERTS // 2):
                        dve.wait_ge(e_fill, n * (1 + SUB * EXPERTS // 2) + 1 + s * EXPERTS // 2 + e2 + 1)
                        for e in (2 * e2, 2 * e2 + 1):
                            src = pE[:, (e2 + 1) % 2, (e % 2) * HID:(e % 2 + 1) * HID]
                            if e == 0:
                                ins = TS(mo[:, s], src, aff[:, s, e:e + 1], None, ALU.mult)
                            else:
                                ins = STT(mo[:, s], src, aff[:, s, e:e + 1], mo[:, s], ALU.mult, ALU.add)
                            if e % 2 == 0:
                                then(ins)
                            elif e < EXPERTS - 1:
                                ins.then_inc(e_read, 1)
                                dve.wait_ge(e_read, n * (1 + SUB * EXPERTS // 2) + 1 + s * EXPERTS // 2 + e2 + 3)
                            else:
                                ins.then_inc(e_read, 1)
                                dve.wait_ge(e_read, n * (1 + SUB * EXPERTS // 2) + 1 + s * EXPERTS // 2 + e2 + 3)
                                dve.sem_inc(mo_done, 1)
                    dve.wait_ge(s_fill, n * SUB + s + 1)
                    dve.wait_ge(out_stored, n * 16 + 16)
                    nc.vector.tensor_copy(s_t[:, s], pS[:, 0:HID]).then_inc(s_read, 1)
                link.restart()

            dve.sem_inc(u_read, 2)
            dve.sem_inc(r_read, 2)
            dve.sem_inc(e_read, 2)
            dve.sem_inc(s_read, 1)
            dve.wait_ge(w_in, NW)
            for k in range(KT):
                TS(w_g[:, k, 0:ND], w_g[:, k, 0:ND], pre[:, k, 0:1], None, ALU.mult).then_inc(w_scaled, 1)
                TS(w_u[:, k, 0:ND], w_u[:, k, 0:ND], pre[:, k, 0:1], None, ALU.mult).then_inc(w_scaled, 1)
                TS(w_g[:, k, ND:], w_g[:, k, ND:], pre[:, k, 1:2], None, ALU.mult).then_inc(w_scaled, 1)
                TS(w_u[:, k, ND:], w_u[:, k, ND:], pre[:, k, 1:2], None, ALU.mult).then_inc(w_scaled, 1)
                TS(w_r[:, k], w_r[:, k], pre[:, k, 2:3], float(HID) ** -0.5, ALU.mult, ALU.mult).then_inc(w_scaled, 1)
            tile(0, False)
            with dve.Fori(0, TILES - 1) as i:
                tile(i + 1, True)
            finish(TILES - 1)
            link.restart()


SCRATCH = {
    "xnT": (P, KT, TOK), "xrT": (P, KT, TOK), "beta": (H, TOK),
    "kq": (BATCH, NCH + 1, P, H, 2 * C), "va": (BATCH, NCH, P, H, 2 * C), "o": (BATCH, NCH, P, H, C),
}


def declare(nc, arrays, shown=()):
    io = {n: nc.dram_tensor("in_" + n, v.shape, mybir.dt.from_np(v.dtype), kind="ExternalInput").ap() for n, v in arrays.items()}
    io["out"] = nc.dram_tensor("out", (TOK, HID), fp32, kind="ExternalOutput").ap()
    scratch = {n: nc.dram_tensor("scr_" + n, s, fp32, kind="ExternalOutput" if n in shown else "Internal").ap() for n, s in SCRATCH.items()}
    return io, scratch


def layouts(i):
    import numpy as np

    def heads(w):
        return np.ascontiguousarray(w.reshape(H, D, -1).transpose(1, 0, 2))

    a = {}
    g = lambda n: np.asarray(i["L0_attn_" + n])
    f = lambda n: np.asarray(i["L0_ffn_" + n])
    a["x"] = g("x").reshape(TOK, HID)
    wall = np.stack([g("Wq"), g("Wk"), g("Wv"), g("Wa")])
    wall = wall.reshape(4, H, D, KT, P).transpose(1, 4, 3, 0, 2).reshape(H, P, KT * 4 * P)
    a["Wqkva"] = np.ascontiguousarray(np.concatenate([wall, wall[-1:]]))
    a["WbT"] = np.ascontiguousarray(g("Wb").T)
    a["bb"] = g("bb").reshape(H, 1)
    a["par"] = np.concatenate([heads(g("qc_w")), heads(g("kc_w")), heads(g("vc_w")), heads(g("qc_b")), heads(g("kc_b")), heads(g("vc_b")), heads(g("ba"))], axis=2)
    a["ident"] = np.eye(P, dtype=np.float32)
    row = np.arange(P)
    a["sel"] = np.ascontiguousarray(np.broadcast_to((row[:, None] % BL == np.arange(BL))[:, :, None], (P, BL, P))).astype(np.float32)
    a["mask"] = np.ascontiguousarray(np.broadcast_to((row[:, None] // BL == np.arange(H))[:, :, None], (P, H, 2 * BL))).astype(np.float32)
    a["rank"] = np.ascontiguousarray(np.broadcast_to(np.arange(EXPERTS, 0, -1), (P, EXPERTS))).astype(np.float32)
    a["cen"] = (np.eye(P) - 1.0 / P).astype(np.float32)
    a["avg"] = np.full((P, 1), 1.0 / P, np.float32)
    a["ln"] = np.stack([g("ln_g"), g("ln_b")], axis=1)
    a["WgT"] = np.ascontiguousarray(g("Wg").T)
    a["WoT"] = np.ascontiguousarray(g("Wo").T)
    a["pre"] = np.stack([f("rn_pre1"), f("rn_pre2"), f("router_scale")], axis=1)
    a["post"] = np.concatenate([f("rn_post1"), f("rn_post2"), f("rn_post")])
    a["pes"] = f("per_expert_scale")
    for n in ("w_gate", "w_up", "w_down", "router_w", "we_gate", "we_up", "we_down"):
        a[n] = f(n)
    return a


def kernel(**inputs):
    import concourse.bacc as _bacc
    from concourse.bass_utils import run_bass_kernel_spmd as _run

    nc = _bacc.Bacc("TRN2", target_bir_lowering=False, num_devices=1)
    arrays = layouts(inputs)
    build(nc, *declare(nc, arrays))
    r = _run(nc, [{"in_" + n: v for n, v in arrays.items()}], core_ids=[0])
    return r.results[0]["out"].reshape(BATCH, SEQ, HID)
```
